# Optimizing a Trainium2 kernel written in Bass

```python
import numpy as np
import jax
import jax.numpy as jnp

def _softmax(x, axis=-1):
    return jax.nn.softmax(x, axis=axis)

def _gelu(x):
    return jax.nn.gelu(x, approximate=True)

def _silu(x):
    return jax.nn.silu(x)

def _sigmoid(x):
    return jax.nn.sigmoid(x)

def _layernorm(x, axis=-1, eps=1e-05):
    m = jnp.mean(x, axis=axis, keepdims=True)
    v = jnp.var(x, axis=axis, keepdims=True)
    return (x - m) / jnp.sqrt(v + eps)

def _scatter_add(tgt, idx, src, axis=0):
    return tgt.at[idx].add(src)

def _segment_sum(src, seg, n):
    return jax.ops.segment_sum(src, seg, n)
kernel_name = 'mk_seq_preln_d1_jaxref_r8_30e4da'

def setup_inputs(seed: int=0):
    np.random.seed(seed)
    _w = jnp.asarray

    def _L0_attn_setup():
        import math
        import jax, jax.numpy as jnp
        import numpy as np
        N_EMBD = 128
        N_HEAD = 16
        HEAD_DIM = N_EMBD // N_HEAD
        key = jax.random.key(seed)
        k1, k2, k3, k4, k5 = jax.random.split(key, 5)
        B, T, C = (1, 512, N_EMBD)
        s = 1.0 / math.sqrt(C)
        return {'x': jax.random.normal(k1, (B, T, C), dtype=jnp.float32), 'w_qkv': jax.random.normal(k2, (C, 3 * C), dtype=jnp.float32) * s, 'b_qkv': jnp.zeros((3 * C,), dtype=jnp.float32), 'w_proj': jax.random.normal(k3, (C, C), dtype=jnp.float32) * s, 'b_proj': jnp.zeros((C,), dtype=jnp.float32)}
    _L0_attn_in = _L0_attn_setup()

    def _L0_ffn_setup():
        import jax, jax.numpy as jnp
        import numpy as np
        B, S, D, H, E = (4, 256, 128, 512, 8)
        THRESHOLD = 0.5
        key = jax.random.key(seed)
        ks = jax.random.split(key, 7)
        s_in = 1.0 / np.sqrt(D)
        s_h = 1.0 / np.sqrt(H)
        return {'x': jax.random.normal(ks[0], (B, S, D), dtype=jnp.float32), 'Wg': jax.random.uniform(ks[1], (D, E), jnp.float32, -s_in, s_in), 'bg': jax.random.uniform(ks[2], (E,), jnp.float32, -s_in, s_in), 'W1': jax.random.uniform(ks[3], (E, D, H), jnp.float32, -s_in, s_in), 'b1': jax.random.uniform(ks[4], (E, H), jnp.float32, -s_in, s_in), 'W2': jax.random.uniform(ks[5], (E, H, D), jnp.float32, -s_h, s_h), 'b2': jax.random.uniform(ks[6], (E, D), jnp.float32, -s_h, s_h)}
    _L0_ffn_in = _L0_ffn_setup()
    _d = {'L0_attn_x': _L0_attn_in['x'], 'L0_attn_w_qkv': _L0_attn_in['w_qkv'], 'L0_attn_b_qkv': _L0_attn_in['b_qkv'], 'L0_attn_w_proj': _L0_attn_in['w_proj'], 'L0_attn_b_proj': _L0_attn_in['b_proj'], 'L0_ffn_Wg': _L0_ffn_in['Wg'], 'L0_ffn_bg': _L0_ffn_in['bg'], 'L0_ffn_W1': _L0_ffn_in['W1'], 'L0_ffn_b1': _L0_ffn_in['b1'], 'L0_ffn_W2': _L0_ffn_in['W2'], 'L0_ffn_b2': _L0_ffn_in['b2']}
    _x0 = _d['L0_attn_x']
    _d['L0_attn_x'] = jax.random.normal(jax.random.fold_in(jax.random.key(seed), 1), (8, 512, 128), dtype=_x0.dtype)
    del _x0
    return _d

def reference(L0_attn_x, L0_attn_w_qkv, L0_attn_b_qkv, L0_attn_w_proj, L0_attn_b_proj, L0_ffn_Wg, L0_ffn_bg, L0_ffn_W1, L0_ffn_b1, L0_ffn_W2, L0_ffn_b2):

    def _L0_attn_ref(x, w_qkv, b_qkv, w_proj, b_proj):
        import math
        import jax, jax.numpy as jnp
        import numpy as np
        N_EMBD = 128
        N_HEAD = 16
        HEAD_DIM = N_EMBD // N_HEAD
        B, T, C = x.shape
        qkv = x @ w_qkv + b_qkv
        q, k, v = jnp.split(qkv, 3, axis=-1)

        def heads(t):
            return t.reshape(B, T, N_HEAD, HEAD_DIM).transpose(0, 2, 1, 3)
        q, k, v = (heads(q), heads(k), heads(v))
        scale = 1.0 / math.sqrt(HEAD_DIM)
        attn = jnp.einsum('bhqd,bhkd->bhqk', q, k) * scale
        causal = jnp.tril(jnp.ones((T, T), dtype=bool))
        attn = jnp.where(causal, attn, -jnp.inf)
        attn = jax.nn.softmax(attn, axis=-1)
        out = jnp.einsum('bhqk,bhkd->bhqd', attn, v)
        out = out.transpose(0, 2, 1, 3).reshape(B, T, C)
        return out @ w_proj + b_proj

    def _L0_ffn_ref(x, Wg, bg, W1, b1, W2, b2):
        import jax, jax.numpy as jnp
        import numpy as np
        B, S, D, H, E = (4, 256, 128, 512, 8)
        THRESHOLD = 0.5
        b, s, d = x.shape
        x_flat = x.reshape(-1, d)
        probs = jax.nn.sigmoid(x_flat @ Wg + bg)
        mask = (probs > THRESHOLD).astype(x_flat.dtype)
        weights = probs * mask
        h = jax.nn.relu(jnp.einsum('td,edh->eth', x_flat, W1) + b1[:, None, :])
        expert_out = jnp.einsum('eth,ehd->etd', h, W2) + b2[:, None, :]
        combined = jnp.einsum('te,etd->td', weights, expert_out)
        return combined.reshape(b, s, d)
    x = L0_attn_x
    x = x + _L0_attn_ref(_layernorm(x, axis=-1), L0_attn_w_qkv, L0_attn_b_qkv, L0_attn_w_proj, L0_attn_b_proj)
    x = x + _L0_ffn_ref(_layernorm(x, axis=-1), L0_ffn_Wg, L0_ffn_bg, L0_ffn_W1, L0_ffn_b1, L0_ffn_W2, L0_ffn_b2)
    return x

_drawn_inputs = setup_inputs


def setup_inputs(seed=0):
    import zlib

    import numpy as np

    out = dict(_drawn_inputs(seed))
    spreads = {'L0_attn_b_qkv': (0.0, 0.1), 'L0_attn_b_proj': (0.0, 0.1)}
    factors = {}
    for name, (base, spread) in spreads.items():
        noise = np.random.default_rng([zlib.crc32(name.encode()), seed]).standard_normal(out[name].shape)
        drawn = base * np.exp(spread * noise) if base else spread * noise
        out[name] = jnp.asarray(drawn.astype(out[name].dtype))
    for name, factor in factors.items():
        out[name] = (out[name] * factor).astype(out[name].dtype)
    return out
```

```python
from contextlib import ExitStack

import numpy as np

import concourse.bass as bass
from concourse import mybir

F32 = mybir.dt.float32
F32R = mybir.dt.float32r
BF16 = mybir.dt.bfloat16
I32 = mybir.dt.int32
ALU = mybir.AluOpType
ACT = mybir.ActivationFunctionType
AX = mybir.AxisListType

BATCH, T, C = 8, 512, 128
HEADS, HD = 16, 8
EXPERTS, HIDDEN = 8, 512
P = 128
TB = T // P
HC = HIDDEN // P
SLOTS = EXPERTS * HC
PAIRS = HEADS // 2
GROUPS, GH = 4, 4
EPS = 1e-5
SCALE = float(HD) ** -0.5
MASKED = -1e38
RSQRT_SEED = 0x5F3759DF
NEWTON = 4

Q_PART = (0, 0, 1, 0, 1, 2)
K_PART = (0, 1, 0, 2, 1, 0)
M_SLOT = 6
STACK_DMAS = 7

MAX_UNITS = ([(3, (j,)) for j in range(GH)] + [(2, (j,)) for j in range(GH)]
             + [(qb, heads) for qb in (1, 0) for heads in ((0, 2), (1, 3))])
EXP_UNITS = []
for _a in (0, 1):
    for _j in (_a, _a + 2):
        EXP_UNITS += [((_j, 0),), ((_j, 1), (_j, 3))]
    EXP_UNITS += [((_a, 2), (_a + 2, 2))]
NMAX, NEXP = len(MAX_UNITS), len(EXP_UNITS)
PT_COL = {piece: u * T + sum((TB - q[1]) * P for q in unit[:n])
          for u, unit in enumerate(EXP_UNITS) for n, piece in enumerate(unit)}


def order_of_work():
    smax = [[("smax", g, u) for u in range(NMAX)] for g in range(GROUPS)]
    sexp = [[("sexp", g, u) for u in range(NEXP)] for g in range(GROUPS)]
    slot = iter(range(SLOTS))

    def ffn(n):
        out = []
        for _ in range(n):
            s = next(slot)
            out += [("z", s)] + ([("y", s - 1)] if s else [])
        return out

    def mix(main, slots):
        out = []
        for n, step in enumerate(main):
            out += [step] + ffn((n + 1) * slots // len(main) - n * slots // len(main))
        return out

    def zipped(a, b):
        out = []
        for n in range(max(len(a), len(b))):
            out += a[n:n + 1] + b[n:n + 1]
        return out

    work = [("gate",), ("ln1",)] + ffn(2) + [("xT",)] + ffn(1) + [("q",), ("k",), ("v",)] + ffn(5)
    work += mix(smax[0], 4)
    work += mix(smax[1][:3] + [("nm", 0)] + smax[1][3:], 4)
    work += mix(zipped(smax[2][:3] + [("nm", 1)] + smax[2][3:], sexp[0]), 4)
    work += mix([("pv", 0)] + zipped(smax[3][:3] + [("nm", 2)] + smax[3][3:], sexp[1]), 4)
    work += mix([("oT", 0), ("pv", 1)] + sexp[2][:2] + [("nm", 3)] + sexp[2][2:], 2)
    work += mix([("oT", 1), ("pv", 2)] + sexp[3], 2)
    work += mix([("oT", 2), ("pv", 3)], 1) + [("oT", 3), ("OT",), ("proj",), ("ln2",)]
    work += ffn(SLOTS - 29) + [("y", SLOTS - 1), ("yT",), ("x2T",)]
    assert next(slot, None) is None
    return work


ORDER = order_of_work()
FFN_STEPS = ("gate", "z", "y", "yT")
ATTENTION = [w for w in ORDER if w[0] not in FFN_STEPS]
EXPERT_WORK = [w for w in ORDER if w[0] in FFN_STEPS]
V_KINDS = ("xT", "q", "k", "v", "smax", "nm", "oT", "OT", "proj", "x2T")
V_UNIT = {w: n for n, w in enumerate(w for w in ATTENTION if w[0] in V_KINDS)}
NV = len(V_UNIT)
NY = EXPERTS + 2
NBR = SLOTS + EXPERTS


def block_program(nc, x, w_qkv, b_qkv, w_proj, b_proj, w_gate, b_gate, w1, b1, w2, b2, out):
    gates_dram = nc.dram_tensor("gates", [EXPERTS, T], F32).ap()

    with ExitStack() as ctx:
        def sb(name, shape, dt=F32):
            return ctx.enter_context(nc.sbuf_tensor(name, shape, dt))

        def bank(name):
            return ctx.enter_context(nc.psum_tensor(name, [P, T], F32))

        def sem(name):
            return ctx.enter_context(nc.semaphore(name))

        ident = sb("ident", [P, P])
        ident16 = sb("ident16", [P, P], BF16)
        mask16 = sb("mask16", [P, P], BF16)
        zeros16 = sb("zeros16", [P, T], BF16)
        wqkv_in = sb("wqkv_in", [P, 3 * C])
        wqk_hi = sb("wqk_hi", [P, 2, C], F32R)
        wqk_lo = sb("wqk_lo", [P, 2, C], F32R)
        bqk = sb("bqk", [P, 2])
        bv = sb("bv", [P, C])
        wp = sb("wp", [P, C])
        bp = sb("bp", [P, C])
        wg_in = sb("wg_in", [P, EXPERTS])
        wg_hi = sb("wg_hi", [P, P], F32R)
        wg_lo = sb("wg_lo", [P, P], F32R)
        bg_in = sb("bg_in", [EXPERTS, 1])
        nbg = sb("nbg", [EXPERTS, 1])
        w1_hi = sb("w1_hi", [P, EXPERTS * HIDDEN], F32R)
        w1_lo = sb("w1_lo", [P, EXPERTS * HIDDEN], F32R)
        w2_sb = sb("w2_sb", [P, SLOTS, C])
        b_rows = sb("b_rows", [NBR, P])
        b_cols = sb("b_cols", [P, NBR])
        b1_sb, b2_sb = b_cols[:, 0:SLOTS], b_cols[:, SLOTS:NBR]

        x_in = sb("x_in", [P, TB, C])
        x_bp = sb("x_bp", [P, TB, C])
        xn = sb("xn", [P, TB, C])
        stats = sb("stats", [P, TB, 6])
        mv = sb("mv", [P, TB, 2])
        var = sb("var", [P, TB])
        hvar = sb("hvar", [P, TB])
        seed = sb("seed", [P, TB], I32)
        rstd = sb("rstd", [P, NEWTON + 1, TB], I32)
        ysq = sb("ysq", [P, TB])
        yv = sb("yv", [P, TB])
        xT = sb("xT", [P, T])
        xT_hi = sb("xT_hi", [P, T], F32R)
        xT_lo = sb("xT_lo", [P, T], F32R)
        parts = sb("parts", [P, 6, T], BF16)
        rest = sb("rest", [P, 2, T])
        stack = sb("stack", [P, PAIRS, 2, T], BF16)
        v_sb = sb("v_sb", [P, TB, HEADS, 32])
        rowmax = sb("rowmax", [P, GROUPS, TB, 2, 2])
        nm16 = sb("nm16", [P, GROUPS, TB, 2, 3, 2], BF16)
        nmr = sb("nmr", [P, GROUPS, TB, 2, 2])
        nmT = sb("nmT", [12, GROUPS, T], BF16)
        pt = sb("pt", [P, 2, NEXP * T])
        o_grp = sb("o_grp", [P, GROUPS, T])
        rden = sb("rden", [P, GROUPS, TB, GH])
        o_tok = sb("o_tok", [P, TB, C])
        oT = sb("oT", [P, T])
        x1 = sb("x1", [P, TB, C])

        x2n = sb("x2n", [P, TB, C])
        x2T = sb("x2T", [P, T])
        x2T_hi = sb("x2T_hi", [P, T], F32R)
        x2T_lo = sb("x2T_lo", [P, T], F32R)
        x1_old = sb("x1_old", [P, TB, C])
        g_exp = sb("g_exp", [EXPERTS, T])
        g_one = g_exp
        g_prob = sb("g_prob", [EXPERTS, T])
        g_w = sb("g_w", [EXPERTS, T])
        wb = sb("wb", [P, EXPERTS, T])
        w1_in = wb
        hid = sb("hid", [P, 2, T])
        term = sb("term", [P, 2, T])
        acc = sb("acc", [P, T])
        o_sb = sb("o_sb", [P, TB, C])

        v_bank = [bank("v_bank0"), bank("v_bank1")]
        e_bank = [bank("e_bank0"), bank("e_bank1")]
        pv_bank = bank("pv_bank")
        z_bank = [bank("z_bank0"), bank("z_bank1")]
        y_bank = bank("y_bank")

        s_wqkv = sem("s_wqkv")
        s_wgt = sem("s_wgt")
        s_w1 = sem("s_w1")
        s_w2 = sem("s_w2")
        s_brow = sem("s_brow")
        s_bT = sem("s_bT")
        s_const = sem("s_const")
        s_vset = sem("s_vset")
        s_w1hi = sem("s_w1hi")
        s_w1lo = sem("s_w1lo")
        s_x = sem("s_x")
        s_xbp = sem("s_xbp")
        s_dve = sem("s_dve")
        s_dvf = sem("s_dvf")
        s_xn = sem("s_xn")
        s_xT = sem("s_xT")
        s_part0 = sem("s_part0")
        s_part = sem("s_part")
        s_stack = sem("s_stack")
        s_vfull = sem("s_vfull")
        s_vfree = sem("s_vfree")
        s_nm = sem("s_nm")
        s_mrow = [sem(f"s_mrow{g}") for g in range(GROUPS)]
        s_efull = sem("s_efull")
        s_exp = sem("s_exp")
        s_mask = sem("s_mask")
        s_pv = sem("s_pv")
        s_og = sem("s_og")
        s_x2n = sem("s_x2n")
        s_x2T = sem("s_x2T")
        s_x1old = sem("s_x1old")
        s_gate = sem("s_gate")
        s_gexp = sem("s_gexp")
        s_gout = sem("s_gout")
        s_wb = sem("s_wb")
        s_z = sem("s_z")
        s_h = sem("s_h")
        s_y = sem("s_y")
        s_yfree = sem("s_yfree")
        s_acc = sem("s_acc")
        s_yT = sem("s_yT")
        s_out = sem("s_out")

        s_apart = {}

        def wait(eng, s, n):
            if not isinstance(n, int) or n > 0:
                eng.wait_ge(s, n)

        def wait_apart(eng, s, n):
            if not isinstance(n, int) or n > 0:
                eng.wait_ge(s, n)
                if not isinstance(n, int):
                    eng.sem_inc(s_apart[id(eng)], 1)

        x_v = x.rearrange("b (t p) c -> b p t c", p=P)
        out_v = out.rearrange("b (t p) c -> b p t c", p=P)
        block = ctx.enter_context(nc.Block())

        def steps_over_sequences(eng, step):
            step(0, ATTENTION)
            with eng.Fori(1, BATCH) as i:
                step(i, ORDER)
            step(BATCH, EXPERT_WORK)

        @block.sync
        def _(sp):
            s_apart[id(sp)] = sem("s_apart_sp")
            sp.dma_start(x_in[:], x_v[0]).then_inc(s_x, 16)
            sp.dma_start(wqkv_in[:], w_qkv).then_inc(s_wqkv, 16)
            for qk in range(2):
                src = b_qkv[qk * C:(qk + 1) * C].rearrange("(n r) -> r n", n=PAIRS)
                sp.dma_start(bqk[:, qk:qk + 1], src,
                             allow_slow_non_contiguous=True).then_inc(s_wqkv, 16)
            sp.dma_start(bv[:], b_qkv[2 * C:].rearrange("(a c) -> a c", a=1)
                         .broadcast_to([P, C])).then_inc(s_wqkv, 16)
            sp.dma_start(bp[:], b_proj.rearrange("(a c) -> a c", a=1)
                         .broadcast_to([P, C])).then_inc(s_wqkv, 16)
            sp.dma_start(wp[:], w_proj).then_inc(s_wqkv, 16)
            sp.dma_start(wg_in[:], w_gate).then_inc(s_wgt, 16)
            sp.dma_start(bg_in[:], b_gate.rearrange("(e a) -> e a", a=1),
                         allow_slow_non_contiguous=True).then_inc(s_wgt, 16)
            sp.dma_start(b_rows[0:SLOTS, :],
                         b1.rearrange("e (c p) -> (e c) p", p=P)).then_inc(s_brow, 16)
            sp.dma_start(b_rows[SLOTS:NBR, :], b2).then_inc(s_brow, 16)
            sp.dma_start(w1_in[:], w1.rearrange("e d h -> d e h")).then_inc(s_w1, 16)
            sp.dma_start(w2_sb[:], w2.rearrange("e (c p) d -> p (e c) d", p=P)).then_inc(s_w2, 16)

            def step(i, work):
                f = i - 1
                for w in work:
                    if w[0] == "gate":
                        wait_apart(sp, s_yfree, f * NY + 1)
                        sp.dma_start(gates_dram, g_w[:]).then_inc(s_gout, 16)
                        wait_apart(sp, s_gout, f * 16 + 16)
                        sp.wait_ge(s_w1lo, 1)
                        sp.dma_start(wb[:], gates_dram.rearrange("(a e) t -> a e t", a=1)
                                     .broadcast_to([P, EXPERTS, T])).then_inc(s_wb, 16)
                    elif w[0] == "v":
                        wait_apart(sp, s_part, i * 2 + 2)
                        wait_apart(sp, s_efull, i * GROUPS * NEXP)
                        if isinstance(i, int) and i == 0:
                            sp.wait_ge(s_const, 11)
                        for s, (a, b) in enumerate(zip(Q_PART, K_PART)):
                            src = parts[:, a:4 + b:3 + b - a, :]
                            sp.dma_start(stack[s::8, :, :, :], src).then_inc(s_stack, 16)
                        sp.dma_start(stack[M_SLOT::8, :, 0, :], zeros16[:]).then_inc(s_stack, 16)
                        if not (isinstance(i, int) and i == BATCH):
                            pass
                    elif w[0] == "nm":
                        g = w[1]
                        wait_apart(sp, s_vfree, i * NV + V_UNIT[w] + 1)
                        for par in range(2):
                            r = 64 * par + M_SLOT
                            sp.dma_start(stack[r:r + 17:8, 2 * g:2 * g + 2, 0, :],
                                         nmT[6 * par:6 * par + 6, g, :]).then_inc(s_mrow[g], 16)
                    elif w[0] == "proj":
                        if isinstance(i, int):
                            nxt = i + 1
                        else:
                            nxt = i + 1
                        wait_apart(sp, s_xn, i * TB + TB)
                        wait_apart(sp, s_xbp, i + 1)
                        sp.dma_start(x_in[:], x_v[bass.ds(nxt, 1)].rearrange("a p t c -> (a p) t c")
                                     if not isinstance(nxt, int) else x_v[nxt]).then_inc(s_x, 16)
                    elif w[0] == "yT":
                        wait_apart(sp, s_yfree, f * NY + NY)
                        dst = out_v[f] if isinstance(f, int) else \
                            out_v[bass.ds(f, 1)].rearrange("a p t c -> (a p) t c")
                        sp.dma_start(dst, o_sb[:]).then_inc(s_out, 16)

            step(0, ATTENTION)
            with sp.Fori(1, BATCH - 1) as i:
                step(i, ORDER)
            step(BATCH - 1, [w for w in ORDER if w[0] != "proj"])
            step(BATCH, EXPERT_WORK)
            sp.wait_ge(s_out, 16 * BATCH)

        @block.gpsimd
        def _(pool):
            s_apart[id(pool)] = sem("s_apart_pool")
            g = nc.gpsimd
            g.memset(ident[:], 0.0).then_inc(s_const, 1)
            g.memset(ident16[:], 0.0).then_inc(s_const, 1)
            g.memset(mask16[:], 0.0).then_inc(s_const, 1)
            g.memset(zeros16[:], 0.0).then_inc(s_const, 1)
            g.memset(stack[:, :, 0, :], 0.0).then_inc(s_const, 1)
            g.memset(stack[:, :, 1, :], 1.0).then_inc(s_const, 1)
            g.memset(v_sb[:], 0.0).then_inc(s_const, 1)
            pool.wait_ge(s_const, 7)
            g.memset(v_sb[:, :, :, HD:HD + 1], 1.0).then_inc(s_const, 1)
            for m in (ident, ident16):
                g.affine_select(out=m[:], in_=m[:], compare_op=ALU.not_equal, fill=1.0, base=0,
                                pattern=[[-1, P]], channel_multiplier=1).then_inc(s_const, 1)
            g.affine_select(out=mask16[:], in_=mask16[:], compare_op=ALU.is_ge, fill=MASKED,
                            base=0, pattern=[[-1, P]], channel_multiplier=1).then_inc(s_const, 1)
            pool.wait_ge(s_w1hi, 1)
            g.tensor_tensor(w1_lo[:], w1_in[:].rearrange("p e h -> p (e h)"),
                            w1_hi[:].bitcast(F32), ALU.subtract).then_inc(s_w1lo, 1)

            def step(i, work):
                f = i - 1
                for w in work:
                    if w[0] == "ln1":
                        wait(pool, s_x, i * 16 + 16)
                        if isinstance(i, int) and i == 0:
                            pool.wait_ge(s_wqkv, 6 * 16)
                        wait(pool, s_vfree, i * NV)
                        g.tensor_tensor(x_bp[:], x_in[:],
                                        bp[:].rearrange("p (a c) -> p a c", a=1)
                                        .broadcast_to([P, TB, C]), ALU.add).then_inc(s_xbp, 1)
                    elif w[0] == "sexp":
                        _, grp, u = w
                        n = grp * NEXP + u
                        wait_apart(pool, s_exp, i * GROUPS * NEXP + n + 1)
                        cols = [PT_COL[piece] for piece in EXP_UNITS[u]]
                        step_ = cols[1] - cols[0] if len(cols) > 1 else P
                        a = pt[:, grp % 2, cols[0]:cols[0] + step_ * (len(cols) - 1) + P]
                        if len(cols) > 1:
                            a = pt[:, grp % 2, u * T:(u + 1) * T]
                            if step_ == 2 * P:
                                a = a.rearrange("p (a c) -> p a c", a=2)[:, :, 0:P]
                            else:
                                a = a.rearrange("p (a c) -> p a c", a=4)[:, 0::3, :]
                        else:
                            a = a.rearrange("p (a c) -> p a c", a=1)
                        g.affine_select(out=a, in_=a, compare_op=ALU.is_ge, fill=0.0, base=0,
                                        pattern=[[0, len(cols)], [1, P]],
                                        channel_multiplier=-1).then_inc(s_mask, 1)
                    elif w[0] == "y" and w[1] % HC == HC - 1 and w[1] >= HC:
                        e = w[1] // HC
                        wait(pool, s_yfree, f * NY + 2 + e)
                        n = f * (EXPERTS - 1) + e - 1
                        if e > 1:
                            wait(pool, s_acc, n)
                        else:
                            wait(pool, s_yT, f)
                        g.tensor_tensor(acc[:], term[:, 0, :] if e == 1 else acc[:],
                                        term[:, e % 2, :], ALU.add).then_inc(s_acc, 1)

            steps_over_sequences(pool, step)

        @block.scalar
        def _(act):
            sc = nc.scalar
            act.wait_ge(s_w1, 16)
            sc.activation(w1_hi[:], w1_in[:].rearrange("p e h -> p (e h)"),
                          ACT.Copy).then_inc(s_w1hi, 1)

            def step(i, work):
                f = i - 1
                for w in work:
                    kind = w[0]
                    if kind == "gate":
                        wait(act, s_gate, f + 1)
                        if isinstance(f, int) and f == BATCH - 1 or not isinstance(f, int):
                            pass
                        wait(act, s_yfree, f * NY)
                        sc.activation(g_exp[:], y_bank[0:EXPERTS, :], ACT.Exp, scale=-1.0,
                                      bias=nbg[:]).then_inc(s_gexp, 1)
                    elif kind in ("q", "k"):
                        qk = int(kind == "k")
                        wait(act, s_vfull, i * NV + V_UNIT[w] + 1)
                        wait(act, s_stack, i * 16 * STACK_DMAS)
                        sc.activation(parts[:, 3 * qk, :], v_bank[V_UNIT[w] % 2][:], ACT.Identity,
                                      bias=bqk[:, qk:qk + 1]).then_inc(s_part0, 1)
                    elif kind == "z":
                        s = w[1]
                        wait(act, s_z, f * SLOTS + s + 1)
                        wait(act, s_y, f * SLOTS + max(s - 1, 0))
                        sc.activation(hid[:, s % 2, :], z_bank[s % 2][:], ACT.Relu,
                                      bias=b1_sb[:, s:s + 1]).then_inc(s_h, 1)
                    elif kind == "sexp":
                        _, grp, u = w
                        n = grp * NEXP + u
                        wait(act, s_efull, i * GROUPS * NEXP + n + 1)
                        if u == 0:
                            wait(act, s_pv, i * GROUPS + grp - 1 if grp else i * GROUPS)
                        sc.activation(pt[:, grp % 2, u * T:(u + 1) * T], e_bank[n % 2][:],
                                      ACT.Exp, scale=SCALE).then_inc(s_exp, 1)
                    elif kind == "pv":
                        grp = w[1]
                        wait(act, s_pv, i * GROUPS + grp + 1)
                        sc.activation(o_grp[:, grp, :], pv_bank[:], ACT.Copy).then_inc(s_og, 1)
                    elif kind == "x2T":
                        wait(act, s_vfree, i * NV + V_UNIT[("proj",)] + 1)
                        wait(act, s_yfree, i * NY)
                        sc.activation(x1_old[:], x1[:], ACT.Copy).then_inc(s_x1old, 1)

            steps_over_sequences(act, step)

        @block.vector
        def _(dve):
            s_apart[id(dve)] = sem("s_apart_dve")
            v = nc.vector
            dve.wait_ge(s_wqkv, 6 * 16)
            for qk in range(2):
                src = wqkv_in[:, qk * C:(qk + 1) * C].rearrange("p (n r) -> p r n", n=PAIRS)
                hi = wqk_hi[:, qk, :].rearrange("p (r n) -> p r n", n=PAIRS)
                v.tensor_copy(hi, src).then_inc(s_vset, 1)
                dve.wait_ge(s_vset, 2 * qk + 1)
                v.tensor_tensor(wqk_lo[:, qk, :].rearrange("p (r n) -> p r n", n=PAIRS), src,
                                hi.bitcast(F32), ALU.subtract).then_inc(s_vset, 1)

            def layernorm(src, dst, done):
                def chained(ins):
                    ins.then_inc(s_dve, 1)
                    chain[0] += 1

                def settle(how=wait):
                    how(dve, s_dve, base[0] + chain[0])

                for t in range(TB):
                    chained(v.bn_stats(stats[:, t, :], src[:, t, :]))
                settle(wait_apart)
                for t in range(TB):
                    chained(v.bn_aggr(mv[:, t, :], stats[:, t, :]))
                settle()
                chained(v.tensor_scalar(var[:], mv[:, :, 1], EPS, None, ALU.add))
                settle()
                chained(v.tensor_scalar(hvar[:], var[:], 0.5, None, ALU.mult))
                chained(v.tensor_scalar(seed[:], var[:].bitcast(I32), 1, None,
                                        ALU.logical_shift_right))
                settle()
                chained(v.tensor_scalar(rstd[:, 0, :], seed[:], -1, RSQRT_SEED, ALU.mult, ALU.add))
                for n in range(NEWTON):
                    y = rstd[:, n, :].bitcast(F32)
                    settle()
                    chained(v.tensor_tensor(ysq[:], y, y, ALU.mult))
                    settle()
                    chained(v.tensor_tensor(yv[:], ysq[:], hvar[:], ALU.mult))
                    settle()
                    chained(v.scalar_tensor_tensor(out=rstd[:, n + 1, :].bitcast(F32), in0=yv[:],
                                                   scalar=1.5, in1=y, op0=ALU.subtract,
                                                   op1=ALU.mult))
                settle()
                for t in range(TB):
                    v.tensor_scalar(dst[:, t, :], src[:, t, :], mv[:, t, 0:1],
                                    rstd[:, NEWTON, t:t + 1].bitcast(F32), ALU.subtract,
                                    ALU.mult).then_inc(done, 1)

            chain, base = [0], [0]
            v.memset(wg_hi[:].bitcast(F32), 0.0).then_inc(s_vset, 1)
            v.memset(wg_lo[:].bitcast(F32), 0.0).then_inc(s_vset, 1)
            dve.wait_ge(s_wgt, 32)
            dve.wait_ge(s_vset, 6)
            v.tensor_copy(wg_hi[:, 0:EXPERTS], wg_in[:]).then_inc(s_vset, 1)
            v.tensor_scalar(nbg[:], bg_in[:], -1.0, None, ALU.mult).then_inc(s_vset, 1)
            dve.wait_ge(s_vset, 8)
            v.tensor_tensor(wg_lo[:, 0:EXPERTS], wg_in[:], wg_hi[:, 0:EXPERTS].bitcast(F32),
                            ALU.subtract).then_inc(s_vset, 1)
            dve.wait_ge(s_bT, 1)
            v.tensor_copy(b_cols[:], y_bank[:, 0:NBR]).then_inc(s_vset, 1)

            def step(i, work):
                f = i - 1
                chain[0] = 0
                base[0] = i * CHAIN
                for w in work:
                    kind = w[0]
                    if kind in V_KINDS:
                        unit = V_UNIT[w]
                        b = v_bank[unit % 2]
                        if kind not in ("q", "k"):
                            wait(dve, s_vfull, i * NV + unit + 1)
                    if kind == "gate":
                        wait(dve, s_gexp, f + 1)
                        v.tensor_scalar(g_one[:], g_exp[:], 1.0, None, ALU.add).then_inc(s_dvf, 1)
                        wait(dve, s_dvf, f * 2 + 1)
                        v.reciprocal(g_prob[:], g_one[:]).then_inc(s_dvf, 1)
                        wait(dve, s_dvf, f * 2 + 2)
                        wait(dve, s_gout, f * 16)
                        v.scalar_tensor_tensor(out=g_w[:], in0=y_bank[0:EXPERTS, :],
                                               scalar=nbg[:], in1=g_prob[:], op0=ALU.is_gt,
                                               op1=ALU.mult).then_inc(s_yfree, 1)
                    elif kind == "ln1":
                        wait(dve, s_x, i * 16 + 16)
                        layernorm(x_in, xn, s_xn)
                    elif kind == "xT":
                        v.tensor_copy(xT[:], b[:]).then_inc(s_vfree, 1)
                        wait(dve, s_vfree, i * NV + unit + 1)
                        v.tensor_copy(xT_hi[:], xT[:]).then_inc(s_dve, 1)
                        chain[0] += 1
                        wait(dve, s_dve, base[0] + chain[0])
                        v.tensor_tensor(xT_lo[:], xT[:], xT_hi[:].bitcast(F32),
                                        ALU.subtract).then_inc(s_xT, 1)
                    elif kind in ("q", "k"):
                        qk = int(kind == "k")
                        wait(dve, s_part0, i * 2 + qk + 1)
                        v.scalar_tensor_tensor(out=rest[:, qk, :], in0=b[:],
                                               scalar=bqk[:, qk:qk + 1], in1=parts[:, 3 * qk, :],
                                               op0=ALU.add, op1=ALU.subtract).then_inc(s_vfree, 1)
                        wait(dve, s_vfree, i * NV + unit + 1)
                        wait(dve, s_stack, i * 16 * STACK_DMAS)
                        v.tensor_copy(parts[:, 3 * qk + 1, :], rest[:, qk, :]).then_inc(s_dve, 1)
                        chain[0] += 1
                        wait(dve, s_dve, base[0] + chain[0])
                        v.tensor_tensor(parts[:, 3 * qk + 2, :], rest[:, qk, :],
                                        parts[:, 3 * qk + 1, :], ALU.subtract).then_inc(s_part, 1)
                    elif kind == "v":
                        wait(dve, s_pv, i * GROUPS)
                        if isinstance(i, int) and i == 0:
                            dve.wait_ge(s_const, 8)
                        v.tensor_tensor(v_sb[:, :, :, 0:HD],
                                        b[:].rearrange("p (t h d) -> p t h d", t=TB, d=HD),
                                        bv[:].rearrange("p (a h d) -> p a h d", a=1, d=HD)
                                        .broadcast_to([P, TB, HEADS, HD]),
                                        ALU.add).then_inc(s_vfree, 1)
                    elif kind == "smax":
                        _, grp, u = w
                        qb, heads = MAX_UNITS[u]
                        width = (qb + 1) * P
                        first, last = heads[0], heads[-1]
                        dst = rowmax[:, grp, qb].rearrange("p r n -> p n r")[
                            :, first // 2:last // 2 + 1, first % 2:last % 2 + 1]
                        v.reduce_max(dst, b[:, 0:width * len(heads)]
                                     .rearrange("p (n r k) -> p n r k", k=width,
                                                n=last // 2 + 1 - first // 2),
                                     AX.X).then_inc(s_vfree, 1)
                        if u == NMAX - 1:
                            wait(dve, s_vfree, i * NV + unit + 1)
                            m, r = rowmax[:, grp], nmr[:, grp]
                            part = [nm16[:, grp, :, :, k, :] for k in range(3)]
                            v.tensor_scalar(part[0], m, -1.0, None, ALU.mult).then_inc(s_dve, 1)
                            chain[0] += 1
                            wait(dve, s_dve, base[0] + chain[0])
                            v.scalar_tensor_tensor(out=r, in0=m, scalar=-1.0, in1=part[0],
                                                   op0=ALU.mult,
                                                   op1=ALU.subtract).then_inc(s_dve, 1)
                            chain[0] += 1
                            wait(dve, s_dve, base[0] + chain[0])
                            v.tensor_copy(part[1], r).then_inc(s_dve, 1)
                            chain[0] += 1
                            wait(dve, s_dve, base[0] + chain[0])
                            v.tensor_tensor(part[2], r, part[1], ALU.subtract).then_inc(s_nm, 1)
                    elif kind == "nm":
                        grp = w[1]
                        wait(dve, s_mrow[grp], i * 32)
                        v.tensor_copy(nmT[:, grp, :], b[:].bitcast(BF16)[0:12, 0:T])\
                            .then_inc(s_vfree, 1)
                    elif kind == "oT":
                        grp = w[1]
                        o = b[:].rearrange("p (t h d) -> p t h d", t=TB, h=GH)
                        v.reciprocal(rden[:, grp], o[:, :, :, HD]).then_inc(s_dve, 1)
                        chain[0] += 1
                        wait(dve, s_dve, base[0] + chain[0])
                        v.tensor_tensor(
                            o_tok[:, :, grp * GH * HD:(grp + 1) * GH * HD]
                            .rearrange("p t (h d) -> p t h d", h=GH),
                            o[:, :, :, 0:HD],
                            rden[:, grp].rearrange("p t (h a) -> p t h a", a=1)
                            .broadcast_to([P, TB, GH, HD]), ALU.mult).then_inc(s_vfree, 1)
                    elif kind == "OT":
                        v.tensor_copy(oT[:], b[:]).then_inc(s_vfree, 1)
                    elif kind == "proj":
                        wait(dve, s_xbp, i + 1)
                        wait(dve, s_x1old, i)
                        v.tensor_tensor(x1[:], b[:].rearrange("p (t c) -> p t c", t=TB), x_bp[:],
                                        ALU.add).then_inc(s_vfree, 1)
                    elif kind == "ln2":
                        wait(dve, s_vfree, i * NV + V_UNIT[("proj",)] + 1)
                        layernorm(x1, x2n, s_x2n)
                    elif kind == "x2T":
                        wait(dve, s_z, i * SLOTS)
                        v.tensor_copy(x2T[:], b[:]).then_inc(s_vfree, 1)
                        wait(dve, s_vfree, i * NV + unit + 1)
                        v.tensor_copy(x2T_hi[:], x2T[:]).then_inc(s_dve, 1)
                        chain[0] += 1
                        wait(dve, s_dve, base[0] + chain[0])
                        v.tensor_tensor(x2T_lo[:], x2T[:], x2T_hi[:].bitcast(F32),
                                        ALU.subtract).then_inc(s_x2T, 1)
                    elif kind == "y" and w[1] % HC == HC - 1:
                        e = w[1] // HC
                        wait(dve, s_y, f * SLOTS + w[1] + 1)
                        if e == 0:
                            wait(dve, s_wb, f * 16 + 16)
                            if isinstance(i, int) and i == BATCH:
                                pass
                        wait(dve, s_acc, f * (EXPERTS - 1) + (max(e - 2, 1) if e > 1 else 0))
                        v.scalar_tensor_tensor(out=term[:, e % 2, :], in0=y_bank[:],
                                               scalar=b2_sb[:, e:e + 1], in1=wb[:, e, :],
                                               op0=ALU.add, op1=ALU.mult).then_inc(s_yfree, 1)
                    elif kind == "yT":
                        wait(dve, s_yT, f + 1)
                        wait(dve, s_x1old, f + 1)
                        wait(dve, s_out, f * 16)
                        v.tensor_tensor(o_sb[:], y_bank[:].rearrange("p (t c) -> p t c", t=TB),
                                        x1_old[:], ALU.add).then_inc(s_yfree, 1)
                assert work is EXPERT_WORK or chain[0] == CHAIN, chain[0]

            steps_over_sequences(dve, step)

        @block.tensor
        def _(pe):
            mm = nc.tensor.matmul

            def split_matmul(dst, hi, lo, x_hi, x_lo):
                mm(dst, hi, x_lo, start=True, stop=False)
                mm(dst, lo, x_hi, start=False, stop=False)
                return mm(dst, hi, x_hi, start=False, stop=True)

            def four_transposes(dst, src, identity):
                for t in range(TB):
                    last = nc.tensor.transpose(dst[:, t * P:(t + 1) * P], src(t), identity)
                return last

            pe.wait_ge(s_const, 11)
            pe.wait_ge(s_brow, 32)
            nc.tensor.transpose(y_bank[:, 0:NBR], b_rows[:], ident[0:NBR, 0:NBR]).then_inc(s_bT, 1)
            pe.wait_ge(s_vset, 10)

            def step(i, work):
                f = i - 1
                for w in work:
                    kind = w[0]
                    if kind in V_KINDS:
                        unit = V_UNIT[w]
                        b = v_bank[unit % 2]
                        wait(pe, s_vfree, i * NV + max(unit - 1, 0))
                    if kind == "gate":
                        wait(pe, s_x2T, f + 1)
                        wait(pe, s_yfree, f * NY)
                        split_matmul(y_bank[:], wg_hi[:], wg_lo[:], x2T_hi[:],
                                     x2T_lo[:]).then_inc(s_gate, 1)
                    elif kind == "xT":
                        wait(pe, s_xn, i * TB + TB)
                        four_transposes(b, lambda t: xn[:, t, :], ident[:]).then_inc(s_vfull, 1)
                    elif kind in ("q", "k"):
                        qk = int(kind == "k")
                        wait(pe, s_xT, i + 1)
                        split_matmul(b[:], wqk_hi[:, qk, :], wqk_lo[:, qk, :], xT_hi[:],
                                     xT_lo[:]).then_inc(s_vfull, 1)
                    elif kind == "v":
                        for t in range(TB):
                            last = mm(b[:, t * P:(t + 1) * P], xT[:, t * P:(t + 1) * P],
                                      wqkv_in[:, 2 * C:], start=True, stop=True)
                        last.then_inc(s_vfull, 1)
                    elif kind == "smax":
                        _, grp, u = w
                        if grp == 0 and u == 0:
                            wait(pe, s_stack, (i + 1) * (16 * STACK_DMAS))
                        qb, heads = MAX_UNITS[u]
                        width = (qb + 1) * P
                        for n, j in enumerate(heads):
                            pair, row = (grp * GH + j) // 2, 64 * (j % 2)
                            rows = stack[row:row + 64, pair]
                            dst = b[:, n * width:(n + 1) * width]
                            mm(dst, rows[:, 0, qb * P:(qb + 1) * P], rows[:, 1, 0:width],
                               start=True, stop=False)
                            last = mm(dst[:, qb * P:], ident16[:], mask16[:], start=False,
                                      stop=True)
                        last.then_inc(s_vfull, 1)
                    elif kind == "nm":
                        grp = w[1]
                        wait(pe, s_nm, i * GROUPS + grp + 1)
                        b16 = b[:].bitcast(BF16)
                        four_transposes(b16[0:12, 0:T],
                                        lambda t: nm16[:, grp, t].rearrange("p r k n -> p (r k n)"),
                                        ident16[:]).then_inc(s_vfull, 1)
                    elif kind == "sexp":
                        _, grp, u = w
                        n = grp * NEXP + u
                        if u == 0:
                            wait(pe, s_mrow[grp], i * 32 + 32)
                        wait(pe, s_exp, i * GROUPS * NEXP + n - 1)
                        col = 0
                        for j, kb in EXP_UNITS[u]:
                            pair, row = (grp * GH + j) // 2, 64 * (j % 2)
                            rows = stack[row:row + 64, pair]
                            width = T - kb * P
                            last = mm(e_bank[n % 2][:, col:col + width],
                                      rows[:, 1, kb * P:(kb + 1) * P], rows[:, 0, kb * P:],
                                      start=True, stop=True)
                            col += width
                        last.then_inc(s_efull, 1)
                    elif kind == "pv":
                        grp = w[1]
                        wait(pe, s_mask, i * GROUPS * NEXP + (grp + 1) * NEXP)
                        wait(pe, s_og, i * GROUPS + grp)
                        for kb in range(TB):
                            for j in range(GH):
                                c = PT_COL[(j, kb)]
                                last = mm(pv_bank[32 * j:32 * j + 32, kb * P:],
                                          v_sb[:, kb, grp * GH + j, :],
                                          pt[:, grp % 2, c:c + T - kb * P], start=(kb == 0),
                                          stop=(kb == TB - 1))
                        last.then_inc(s_pv, 1)
                    elif kind == "oT":
                        grp = w[1]
                        wait(pe, s_og, i * GROUPS + grp + 1)
                        four_transposes(b, lambda t: o_grp[:, grp, t * P:(t + 1) * P],
                                        ident[:]).then_inc(s_vfull, 1)
                    elif kind == "OT":
                        wait(pe, s_vfree, i * NV + unit)
                        four_transposes(b, lambda t: o_tok[:, t, :], ident[:]).then_inc(s_vfull, 1)
                    elif kind == "proj":
                        wait(pe, s_vfree, i * NV + unit)
                        for t in range(TB):
                            last = mm(b[:, t * P:(t + 1) * P], oT[:, t * P:(t + 1) * P], wp[:],
                                      start=True, stop=True)
                        last.then_inc(s_vfull, 1)
                    elif kind == "x2T":
                        wait(pe, s_x2n, i * TB + TB)
                        four_transposes(b, lambda t: x2n[:, t, :], ident[:]).then_inc(s_vfull, 1)
                    elif kind == "z":
                        s = w[1]
                        if s == 0:
                            if not isinstance(i, int) or i == 1:
                                pe.wait_ge(s_w1lo, 1)
                        wait(pe, s_h, f * SLOTS + max(s - 1, 0))
                        split_matmul(z_bank[s % 2][:], w1_hi[:, s * P:(s + 1) * P],
                                     w1_lo[:, s * P:(s + 1) * P], x2T_hi[:],
                                     x2T_lo[:]).then_inc(s_z, 1)
                    elif kind == "y":
                        s = w[1]
                        wait(pe, s_h, f * SLOTS + s + 1)
                        if s % HC == 0:
                            wait(pe, s_yfree, f * NY + 1 + s // HC)
                        mm(y_bank[:], w2_sb[:, s, :], hid[:, s % 2, :], start=(s % HC == 0),
                           stop=(s % HC == HC - 1)).then_inc(s_y, 1)
                    elif kind == "yT":
                        wait(pe, s_acc, f * (EXPERTS - 1) + EXPERTS - 1)
                        wait(pe, s_yfree, f * NY + 1 + EXPERTS)
                        four_transposes(y_bank, lambda t: acc[:, t * P:(t + 1) * P],
                                        ident[:]).then_inc(s_yT, 1)

            pe.wait_ge(s_w2, 16)
            steps_over_sequences(pe, step)


CHAIN = 2 * (2 * TB + 4 + 3 * NEWTON) + 2 + 2 + 3 * GROUPS + GROUPS


_INS = ["L0_attn_x", "L0_attn_w_qkv", "L0_attn_b_qkv", "L0_attn_w_proj", "L0_attn_b_proj",
        "L0_ffn_Wg", "L0_ffn_bg", "L0_ffn_W1", "L0_ffn_b1", "L0_ffn_W2", "L0_ffn_b2"]


def kernel(**inputs):
    import concourse.bacc as bacc
    from concourse.bass_utils import run_bass_kernel_spmd

    nc = bacc.Bacc("TRN2", target_bir_lowering=False, num_devices=1)
    arrays, args = {}, []
    for name in _INS:
        a = np.ascontiguousarray(inputs[name])
        arrays[f"in_{name}"] = a
        args.append(nc.dram_tensor(f"in_{name}", a.shape, mybir.dt.from_np(a.dtype),
                                   kind="ExternalInput").ap())
    out = nc.dram_tensor("out_x", (BATCH, T, C), F32, kind="ExternalOutput").ap()
    block_program(nc, *args, out)
    result = run_bass_kernel_spmd(nc, [arrays], core_ids=[0])
    return result.results[0]["out_x"]
```

```python
from contextlib import ExitStack

import numpy as np

import concourse.bass as bass
from concourse import mybir

F32 = mybir.dt.float32
F32R = mybir.dt.float32r
BF16 = mybir.dt.bfloat16
I32 = mybir.dt.int32
ALU = mybir.AluOpType
ACT = mybir.ActivationFunctionType
AX = mybir.AxisListType

BATCH, T, C = 8, 512, 128
HEADS, HD = 16, 8
EXPERTS, HIDDEN = 8, 512
P = 128
TB = T // P
HC = HIDDEN // P
SLOTS = EXPERTS * HC
PAIRS = HEADS // 2
GROUPS, GH = 4, 4
EPS = 1e-5
SCALE = float(HD) ** -0.5
MASKED = -1e38
RSQRT_SEED = 0x5F3759DF
NEWTON = 4

Q_PART = (0, 0, 1, 0, 1, 2)
K_PART = (0, 1, 0, 2, 1, 0)
M_SLOT = 6
STACK_DMAS = 7

MAX_UNITS = ([(3, (j,)) for j in range(GH)] + [(2, (j,)) for j in range(GH)]
             + [(qb, heads) for qb in (1, 0) for heads in ((0, 2), (1, 3))])
EXP_UNITS = []
for _a in (0, 1):
    for _j in (_a, _a + 2):
        EXP_UNITS += [((_j, 0),), ((_j, 1), (_j, 3))]
    EXP_UNITS += [((_a, 2), (_a + 2, 2))]
NMAX, NEXP = len(MAX_UNITS), len(EXP_UNITS)
PT_COL = {piece: u * T + sum((TB - q[1]) * P for q in unit[:n])
          for u, unit in enumerate(EXP_UNITS) for n, piece in enumerate(unit)}


def order_of_work():
    smax = [[("smax", g, u) for u in range(NMAX)] for g in range(GROUPS)]
    sexp = [[("sexp", g, u) for u in range(NEXP)] for g in range(GROUPS)]
    experts = [("z", 0)]
    for s in range(1, SLOTS):
        experts += [("z", s), ("y", s - 1)]
    experts += [("y", SLOTS - 1)]
    experts = iter(experts)

    def mix(main, n):
        out = []
        for k, step in enumerate(main):
            out += [step] + [next(experts) for _ in range((k + 1) * n // len(main)
                                                          - k * n // len(main))]
        return out

    def zipped(a, b):
        out = []
        for n in range(max(len(a), len(b))):
            out += a[n:n + 1] + b[n:n + 1]
        return out

    work = [("xbp",), ("xload",)] + smax[0][:4] + [("gate",)]
    work += mix(smax[0][4:], 6)
    work += mix(smax[1][:4] + [("nm", 0)] + smax[1][4:], 10)
    work += mix(zipped(smax[2][:4] + [("nm", 1)] + smax[2][4:], sexp[0]), 10)
    phase = zipped(smax[3][:4] + [("nm", 2)] + smax[3][4:], sexp[1])
    work += mix(phase[:8] + [("pv", 0)] + phase[8:], 11)
    work += mix([("oT", 0)] + sexp[2][:3] + [("nm", 3), ("pv", 1)] + sexp[2][3:], 6)
    work += [("ln1",)] + mix([("oT", 1)] + sexp[3][:3] + [("pv", 2)] + sexp[3][3:], 6)
    work += mix([("oT", 2), ("xT",), ("pv", 3), ("q",), ("k",), ("oT", 3), ("OT",), ("v",)], 6)
    work += [("stack",), ("proj",), ("ln2",)]
    work += list(experts) + [("x2T",), ("yT",), ("keep",)]
    return work


ORDER = order_of_work()
EXPERT_KINDS = ("gate", "z", "y", "yT")
NEXT_KINDS = ("xload", "ln1", "xT", "q", "k", "v", "stack")
FIRST_PREP = [("ln1",), ("xT",), ("q",), ("k",), ("v",), ("stack",)]
FIRST = [w for w in ORDER if w[0] not in EXPERT_KINDS]
LAST = [w for w in ORDER if w[0] not in NEXT_KINDS]
EXPERT_WORK = [w for w in ORDER if w[0] in EXPERT_KINDS]
V_KINDS = ("xT", "q", "k", "v", "smax", "nm", "oT", "OT", "proj", "x2T")


def turn(work):
    return {w: n for n, w in enumerate(w for w in work if w[0] in V_KINDS)}


CHAIN_NORM = 2 * TB + 4 + 3 * NEWTON
CHAIN_PREP = CHAIN_NORM + 3
CHAIN = CHAIN_PREP + CHAIN_NORM + 1 + 3 * GROUPS + GROUPS
NV_PREP, NV = len(turn(FIRST_PREP)), len(turn(ORDER))
NY = EXPERTS + 1
NBR = SLOTS + EXPERTS


def block_program(nc, x, w_qkv, b_qkv, w_proj, b_proj, w_gate, b_gate, w1, b1, w2, b2, out):
    gates_dram = nc.dram_tensor("gates", [EXPERTS, T], F32).ap()

    with ExitStack() as ctx:
        def sb(name, shape, dt=F32):
            return ctx.enter_context(nc.sbuf_tensor(name, shape, dt))

        def bank(name):
            return ctx.enter_context(nc.psum_tensor(name, [P, T], F32))

        def sem(name):
            return ctx.enter_context(nc.semaphore(name))

        ident = sb("ident", [P, P])
        ident16 = sb("ident16", [P, P], BF16)
        mask16 = sb("mask16", [P, P], BF16)
        zeros16 = sb("zeros16", [P, T], BF16)
        wqkv_in = sb("wqkv_in", [P, 3 * C])
        wqk_hi = sb("wqk_hi", [P, 2, C], F32R)
        wqk_lo = sb("wqk_lo", [P, 2, C], F32R)
        bqk = sb("bqk", [P, 2])
        bv = sb("bv", [P, C])
        wp = sb("wp", [P, C])
        bp = sb("bp", [P, C])
        wg_in = sb("wg_in", [P, EXPERTS])
        wg_hi = sb("wg_hi", [P, P], F32R)
        wg_lo = sb("wg_lo", [P, P], F32R)
        bg_in = sb("bg_in", [EXPERTS, 1])
        hbg = sb("hbg", [EXPERTS, 1])
        w1_hi = sb("w1_hi", [P, EXPERTS * HIDDEN], F32R)
        w1_lo = sb("w1_lo", [P, EXPERTS * HIDDEN], F32R)
        w2_sb = sb("w2_sb", [P, SLOTS, C])
        b_rows = sb("b_rows", [NBR, P])
        b_cols = sb("b_cols", [P, NBR])
        b1_sb, b2_sb = b_cols[:, 0:SLOTS], b_cols[:, SLOTS:NBR]

        x_in = sb("x_in", [P, TB, C])
        x_bp = sb("x_bp", [P, TB, C])
        xn = sb("xn", [P, TB, C])
        stats = sb("stats", [P, TB, 6])
        mv = sb("mv", [P, TB, 2])
        var = sb("var", [P, TB])
        hvar = sb("hvar", [P, TB])
        seed = sb("seed", [P, TB], I32)
        rstd = sb("rstd", [P, NEWTON + 1, TB], I32)
        ysq = sb("ysq", [P, TB])
        yv = sb("yv", [P, TB])
        xT = sb("xT", [P, T])
        xT_hi = sb("xT_hi", [P, T], F32R)
        xT_lo = sb("xT_lo", [P, T], F32R)
        parts = sb("parts", [P, 6, T], BF16)
        rest = sb("rest", [P, 2, T])
        stack = sb("stack", [P, PAIRS, 2, T], BF16)
        v_sb = sb("v_sb", [P, TB, HEADS, 32])
        rowmax = sb("rowmax", [P, GROUPS, TB, 2, 2])
        nm16 = sb("nm16", [P, GROUPS, TB, 2, 3, 2], BF16)
        nmr = sb("nmr", [P, GROUPS, TB, 2, 2])
        nmT = sb("nmT", [12, GROUPS, T], BF16)
        pt = sb("pt", [P, 2, NEXP * T])
        o_grp = sb("o_grp", [P, GROUPS, T])
        rden = sb("rden", [P, GROUPS, TB, GH])
        o_tok = sb("o_tok", [P, TB, C])
        oT = sb("oT", [P, T])
        x1 = sb("x1", [P, TB, C])

        x2n = sb("x2n", [P, TB, C])
        x2T = sb("x2T", [P, T])
        x2T_hi = sb("x2T_hi", [P, T], F32R)
        x2T_lo = sb("x2T_lo", [P, T], F32R)
        x1_old = sb("x1_old", [P, TB, C])
        g_tanh = sb("g_tanh", [EXPERTS, T])
        g_prob = sb("g_prob", [EXPERTS, T])
        g_w = sb("g_w", [EXPERTS, T])
        wb = sb("wb", [P, EXPERTS, T])
        w1_in = wb
        hid = sb("hid", [P, 2, T])
        term = sb("term", [P, 2, T])
        acc = sb("acc", [P, T])
        o_sb = sb("o_sb", [P, TB, C])

        v_bank = [bank("v_bank0"), bank("v_bank1")]
        e_bank = [bank("e_bank0"), bank("e_bank1")]
        pv_bank = bank("pv_bank")
        z_bank = [bank("z_bank0"), bank("z_bank1")]
        y_bank = bank("y_bank")

        s_wqkv = sem("s_wqkv")
        s_wgt = sem("s_wgt")
        s_w1 = sem("s_w1")
        s_w2 = sem("s_w2")
        s_brow = sem("s_brow")
        s_bT = sem("s_bT")
        s_const = sem("s_const")
        s_vset = sem("s_vset")
        s_w1hi = sem("s_w1hi")
        s_w1lo = sem("s_w1lo")
        s_x = sem("s_x")
        s_xbp = sem("s_xbp")
        s_dve = sem("s_dve")
        s_xn = sem("s_xn")
        s_xT = sem("s_xT")
        s_part0 = sem("s_part0")
        s_part = sem("s_part")
        s_stack = sem("s_stack")
        s_vfull = sem("s_vfull")
        s_vfree = sem("s_vfree")
        s_nm = sem("s_nm")
        s_mrow = [sem(f"s_mrow{g}") for g in range(GROUPS)]
        s_efull = sem("s_efull")
        s_exp = sem("s_exp")
        s_mask = sem("s_mask")
        s_pv = sem("s_pv")
        s_og = sem("s_og")
        s_x2n = sem("s_x2n")
        s_x2T = sem("s_x2T")
        s_x1old = sem("s_x1old")
        s_gate = sem("s_gate")
        s_gtanh = sem("s_gtanh")
        s_gprob = sem("s_gprob")
        s_gw = sem("s_gw")
        s_gout = sem("s_gout")
        s_wb = [sem("s_wb0"), sem("s_wb1")]
        s_z = sem("s_z")
        s_h = sem("s_h")
        s_y = sem("s_y")
        s_yfree = sem("s_yfree")
        s_acc = sem("s_acc")
        s_yT = sem("s_yT")
        s_out = sem("s_out")

        s_apart = {}

        primed = (s_h, s_y, s_yfree, s_gw, s_gout, s_acc, s_yT, s_out)

        def wait(eng, s, n):
            if not isinstance(n, int) or n > 0:
                eng.wait_ge(s, n + 1 if s in primed else n)

        def wait_apart(eng, s, n):
            if not isinstance(n, int) or n > 0:
                wait(eng, s, n)
                if not isinstance(n, int):
                    eng.sem_inc(s_apart[id(eng)], 1)

        x_v = x.rearrange("b (t p) c -> b p t c", p=P)
        out_v = out.rearrange("b (t p) c -> b p t c", p=P)
        block = ctx.enter_context(nc.Block())

        def steps_over_sequences(eng, step):
            step(-1, FIRST_PREP)
            step(0, FIRST)
            with eng.Fori(1, BATCH - 1) as i:
                step(i, ORDER)
            step(BATCH - 1, LAST)
            step(BATCH, EXPERT_WORK)

        def v_count(i):
            return 0 if isinstance(i, int) and i < 0 else NV_PREP + i * NV

        @block.sync
        def _(sp):
            s_apart[id(sp)] = sem("s_apart_sp")
            for s in primed:
                sp.sem_inc(s, 1)
            sp.dma_start(x_in[:], x_v[0]).then_inc(s_x, 16)
            sp.dma_start(wqkv_in[:], w_qkv).then_inc(s_wqkv, 16)
            for qk in range(2):
                src = b_qkv[qk * C:(qk + 1) * C].rearrange("(n r) -> r n", n=PAIRS)
                sp.dma_start(bqk[:, qk:qk + 1], src,
                             allow_slow_non_contiguous=True).then_inc(s_wqkv, 16)
            sp.dma_start(bv[:], b_qkv[2 * C:].rearrange("(a c) -> a c", a=1)
                         .broadcast_to([P, C])).then_inc(s_wqkv, 16)
            sp.dma_start(bp[:], b_proj.rearrange("(a c) -> a c", a=1)
                         .broadcast_to([P, C])).then_inc(s_wqkv, 16)
            sp.dma_start(wp[:], w_proj).then_inc(s_wqkv, 16)
            sp.dma_start(wg_in[:], w_gate).then_inc(s_wgt, 16)
            sp.dma_start(bg_in[:], b_gate.rearrange("(e a) -> e a", a=1),
                         allow_slow_non_contiguous=True).then_inc(s_wgt, 16)
            sp.dma_start(b_rows[0:SLOTS, :],
                         b1.rearrange("e (c p) -> (e c) p", p=P)).then_inc(s_brow, 16)
            sp.dma_start(b_rows[SLOTS:NBR, :], b2).then_inc(s_brow, 16)
            sp.dma_start(w1_in[:], w1.rearrange("e d h -> d e h")).then_inc(s_w1, 16)
            sp.dma_start(w2_sb[:], w2.rearrange("e (c p) d -> p (e c) d", p=P)).then_inc(s_w2, 16)

            def step(i, work):
                f, nxt, unit, first = i - 1, i + 1, turn(work), v_count(i)
                for w in work:
                    if w[0] == "gate":
                        wait_apart(sp, s_gw, f + 1)
                        sp.dma_start(gates_dram, g_w[:]).then_inc(s_gout, 16)
                        wait_apart(sp, s_gout, f * 16 + 16)
                        sp.wait_ge(s_w1lo, 1)
                        wait_apart(sp, s_yfree, f * NY)
                        for half, (e0, e1) in enumerate(((0, 2), (2, EXPERTS))):
                            sp.dma_start(wb[:, e0:e1],
                                         gates_dram[e0:e1].rearrange("(a e) t -> a e t", a=1)
                                         .broadcast_to([P, e1 - e0, T])).then_inc(s_wb[half], 16)
                    elif w[0] == "stack":
                        wait_apart(sp, s_part, nxt * 2 + 2)
                        wait_apart(sp, s_efull, nxt * GROUPS * NEXP)
                        if isinstance(i, int) and i < 0:
                            sp.wait_ge(s_const, 11)
                        for s, (a, b) in enumerate(zip(Q_PART, K_PART)):
                            src = parts[:, a:4 + b:3 + b - a, :]
                            sp.dma_start(stack[s::8, :, :, :], src).then_inc(s_stack, 16)
                        sp.dma_start(stack[M_SLOT::8, :, 0, :], zeros16[:]).then_inc(s_stack, 16)
                    elif w[0] == "nm":
                        g = w[1]
                        wait_apart(sp, s_vfree, first + unit[w] + 1)
                        for par in range(2):
                            r = 64 * par + M_SLOT
                            sp.dma_start(stack[r:r + 17:8, 2 * g:2 * g + 2, 0, :],
                                         nmT[6 * par:6 * par + 6, g, :]).then_inc(s_mrow[g], 16)
                    elif w[0] == "xload":
                        wait_apart(sp, s_xn, i * TB + TB)
                        wait_apart(sp, s_xbp, i + 1)
                        src = x_v[nxt] if isinstance(nxt, int) else \
                            x_v[bass.ds(nxt, 1)].rearrange("a p t c -> (a p) t c")
                        sp.dma_start(x_in[:], src).then_inc(s_x, 16)
                    elif w[0] == "yT":
                        wait_apart(sp, s_yfree, f * NY + NY)
                        dst = out_v[f] if isinstance(f, int) else \
                            out_v[bass.ds(f, 1)].rearrange("a p t c -> (a p) t c")
                        sp.dma_start(dst, o_sb[:]).then_inc(s_out, 16)

            steps_over_sequences(sp, step)
            wait(sp, s_out, 16 * BATCH)

        @block.gpsimd
        def _(pool):
            s_apart[id(pool)] = sem("s_apart_pool")
            g = nc.gpsimd
            g.memset(ident[:], 0.0).then_inc(s_const, 1)
            g.memset(ident16[:], 0.0).then_inc(s_const, 1)
            g.memset(mask16[:], 0.0).then_inc(s_const, 1)
            g.memset(zeros16[:], 0.0).then_inc(s_const, 1)
            g.memset(stack[:, :, 0, :], 0.0).then_inc(s_const, 1)
            g.memset(stack[:, :, 1, :], 1.0).then_inc(s_const, 1)
            g.memset(v_sb[:], 0.0).then_inc(s_const, 1)
            pool.wait_ge(s_const, 7)
            g.memset(v_sb[:, :, :, HD:HD + 1], 1.0).then_inc(s_const, 1)
            for m in (ident, ident16):
                g.affine_select(out=m[:], in_=m[:], compare_op=ALU.not_equal, fill=1.0, base=0,
                                pattern=[[-1, P]], channel_multiplier=1).then_inc(s_const, 1)
            g.affine_select(out=mask16[:], in_=mask16[:], compare_op=ALU.is_ge, fill=MASKED,
                            base=0, pattern=[[-1, P]], channel_multiplier=1).then_inc(s_const, 1)
            pool.wait_ge(s_w1hi, 1)
            g.tensor_tensor(w1_lo[:], w1_in[:].rearrange("p e h -> p (e h)"),
                            w1_hi[:].bitcast(F32), ALU.subtract).then_inc(s_w1lo, 1)

            def step(i, work):
                f = i - 1
                for w in work:
                    if w[0] == "xbp":
                        wait(pool, s_x, i * 16 + 16)
                        if isinstance(i, int) and i == 0:
                            pool.wait_ge(s_wqkv, 6 * 16)
                        wait(pool, s_vfree, v_count(i))
                        g.tensor_tensor(x_bp[:], x_in[:],
                                        bp[:].rearrange("p (a c) -> p a c", a=1)
                                        .broadcast_to([P, TB, C]), ALU.add).then_inc(s_xbp, 1)
                    elif w[0] == "sexp":
                        _, grp, u = w
                        n = grp * NEXP + u
                        wait_apart(pool, s_exp, i * GROUPS * NEXP + n + 1)
                        cols = [PT_COL[piece] for piece in EXP_UNITS[u]]
                        step_ = cols[1] - cols[0] if len(cols) > 1 else P
                        a = pt[:, grp % 2, cols[0]:cols[0] + step_ * (len(cols) - 1) + P]
                        if len(cols) > 1:
                            a = pt[:, grp % 2, u * T:(u + 1) * T]
                            if step_ == 2 * P:
                                a = a.rearrange("p (a c) -> p a c", a=2)[:, :, 0:P]
                            else:
                                a = a.rearrange("p (a c) -> p a c", a=4)[:, 0::3, :]
                        else:
                            a = a.rearrange("p (a c) -> p a c", a=1)
                        g.affine_select(out=a, in_=a, compare_op=ALU.is_ge, fill=0.0, base=0,
                                        pattern=[[0, len(cols)], [1, P]],
                                        channel_multiplier=-1).then_inc(s_mask, 1)
                    elif w[0] == "y" and w[1] % HC == HC - 1 and w[1] >= HC:
                        e = w[1] // HC
                        wait(pool, s_yfree, f * NY + 1 + e)
                        n = f * (EXPERTS - 1) + e - 1
                        if e > 1:
                            wait(pool, s_acc, n)
                        else:
                            wait(pool, s_yT, f)
                        g.tensor_tensor(acc[:], term[:, 0, :] if e == 1 else acc[:],
                                        term[:, e % 2, :], ALU.add).then_inc(s_acc, 1)

            steps_over_sequences(pool, step)

        @block.scalar
        def _(act):
            sc = nc.scalar
            act.wait_ge(s_w1, 16)
            sc.activation(w1_hi[:], w1_in[:].rearrange("p e h -> p (e h)"),
                          ACT.Copy).then_inc(s_w1hi, 1)

            def step(i, work):
                f, nxt, unit, first = i - 1, i + 1, turn(work), v_count(i)
                for w in work:
                    kind = w[0]
                    if kind == "gate":
                        wait(act, s_gate, f + 1)
                        wait(act, s_gw, f)
                        sc.activation(g_tanh[:], y_bank[0:EXPERTS, :], ACT.Tanh, scale=0.5,
                                      bias=hbg[:]).then_inc(s_gtanh, 1)
                    elif kind in ("q", "k"):
                        qk = int(kind == "k")
                        wait(act, s_vfull, first + unit[w] + 1)
                        wait(act, s_stack, nxt * 16 * STACK_DMAS)
                        sc.activation(parts[:, 3 * qk, :], v_bank[unit[w] % 2][:], ACT.Identity,
                                      bias=bqk[:, qk:qk + 1]).then_inc(s_part0, 1)
                    elif kind == "z":
                        s = w[1]
                        wait(act, s_z, f * SLOTS + s + 1)
                        wait(act, s_y, f * SLOTS + max(s - 1, 0))
                        sc.activation(hid[:, s % 2, :], z_bank[s % 2][:], ACT.Relu,
                                      bias=b1_sb[:, s:s + 1]).then_inc(s_h, 1)
                    elif kind == "sexp":
                        _, grp, u = w
                        n = grp * NEXP + u
                        wait(act, s_efull, i * GROUPS * NEXP + n + 1)
                        if u == 0:
                            wait(act, s_pv, i * GROUPS + grp - 1 if grp else i * GROUPS)
                        sc.activation(pt[:, grp % 2, u * T:(u + 1) * T], e_bank[n % 2][:],
                                      ACT.Exp, scale=SCALE).then_inc(s_exp, 1)
                    elif kind == "pv":
                        grp = w[1]
                        wait(act, s_pv, i * GROUPS + grp + 1)
                        sc.activation(o_grp[:, grp, :], pv_bank[:], ACT.Copy).then_inc(s_og, 1)
                    elif kind == "keep":
                        wait(act, s_vfree, first + unit[("proj",)] + 1)
                        wait(act, s_yfree, i * NY)
                        sc.activation(x1_old[:], x1[:], ACT.Copy).then_inc(s_x1old, 1)

            steps_over_sequences(act, step)

        @block.vector
        def _(dve):
            s_apart[id(dve)] = sem("s_apart_dve")
            v = nc.vector
            dve.wait_ge(s_wqkv, 6 * 16)
            for qk in range(2):
                src = wqkv_in[:, qk * C:(qk + 1) * C].rearrange("p (n r) -> p r n", n=PAIRS)
                hi = wqk_hi[:, qk, :].rearrange("p (r n) -> p r n", n=PAIRS)
                v.tensor_copy(hi, src).then_inc(s_vset, 1)
                dve.wait_ge(s_vset, 2 * qk + 1)
                v.tensor_tensor(wqk_lo[:, qk, :].rearrange("p (r n) -> p r n", n=PAIRS), src,
                                hi.bitcast(F32), ALU.subtract).then_inc(s_vset, 1)

            def layernorm(src, dst, done):
                def chained(ins):
                    ins.then_inc(s_dve, 1)
                    chain[0] += 1

                def settle(how=wait):
                    how(dve, s_dve, base[0] + chain[0])

                for t in range(TB):
                    chained(v.bn_stats(stats[:, t, :], src[:, t, :]))
                settle(wait_apart)
                for t in range(TB):
                    chained(v.bn_aggr(mv[:, t, :], stats[:, t, :]))
                settle()
                chained(v.tensor_scalar(var[:], mv[:, :, 1], EPS, None, ALU.add))
                settle()
                chained(v.tensor_scalar(hvar[:], var[:], 0.5, None, ALU.mult))
                chained(v.tensor_scalar(seed[:], var[:].bitcast(I32), 1, None,
                                        ALU.logical_shift_right))
                settle()
                chained(v.tensor_scalar(rstd[:, 0, :], seed[:], -1, RSQRT_SEED, ALU.mult, ALU.add))
                for n in range(NEWTON):
                    y = rstd[:, n, :].bitcast(F32)
                    settle()
                    chained(v.tensor_tensor(ysq[:], y, y, ALU.mult))
                    settle()
                    chained(v.tensor_tensor(yv[:], ysq[:], hvar[:], ALU.mult))
                    settle()
                    chained(v.scalar_tensor_tensor(out=rstd[:, n + 1, :].bitcast(F32), in0=yv[:],
                                                   scalar=1.5, in1=y, op0=ALU.subtract,
                                                   op1=ALU.mult))
                settle()
                for t in range(TB):
                    v.tensor_scalar(dst[:, t, :], src[:, t, :], mv[:, t, 0:1],
                                    rstd[:, NEWTON, t:t + 1].bitcast(F32), ALU.subtract,
                                    ALU.mult).then_inc(done, 1)

            chain, base = [0], [0]
            v.memset(wg_hi[:].bitcast(F32), 0.0).then_inc(s_vset, 1)
            v.memset(wg_lo[:].bitcast(F32), 0.0).then_inc(s_vset, 1)
            dve.wait_ge(s_wgt, 32)
            dve.wait_ge(s_vset, 6)
            v.tensor_copy(wg_hi[:, 0:EXPERTS], wg_in[:]).then_inc(s_vset, 1)
            v.tensor_scalar(hbg[:], bg_in[:], 0.5, None, ALU.mult).then_inc(s_vset, 1)
            dve.wait_ge(s_vset, 8)
            v.tensor_tensor(wg_lo[:, 0:EXPERTS], wg_in[:], wg_hi[:, 0:EXPERTS].bitcast(F32),
                            ALU.subtract).then_inc(s_vset, 1)
            dve.wait_ge(s_bT, 1)
            v.tensor_copy(b_cols[:], y_bank[:, 0:NBR]).then_inc(s_vset, 1)

            def step(i, work):
                f, nxt, units, first = i - 1, i + 1, turn(work), v_count(i)
                chain[0] = 0
                base[0] = 0 if isinstance(i, int) and i < 0 else CHAIN_PREP + i * CHAIN
                for w in work:
                    kind = w[0]
                    if kind in V_KINDS:
                        unit = first + units[w]
                        b = v_bank[units[w] % 2]
                        if kind not in ("q", "k"):
                            wait(dve, s_vfull, unit + 1)
                    if kind == "gate":
                        wait(dve, s_gtanh, f + 1)
                        v.tensor_scalar(g_prob[:], g_tanh[:], 0.5, 0.5, ALU.mult,
                                        ALU.add).then_inc(s_gprob, 1)
                        wait(dve, s_gprob, f + 1)
                        wait(dve, s_gout, f * 16)
                        v.scalar_tensor_tensor(out=g_w[:], in0=g_tanh[:], scalar=0.0,
                                               in1=g_prob[:], op0=ALU.is_gt,
                                               op1=ALU.mult).then_inc(s_gw, 1)
                    elif kind == "ln1":
                        wait(dve, s_x, nxt * 16 + 16)
                        layernorm(x_in, xn, s_xn)
                    elif kind == "xT":
                        v.tensor_copy(xT[:], b[:]).then_inc(s_vfree, 1)
                        wait(dve, s_vfree, unit + 1)
                        v.tensor_copy(xT_hi[:], xT[:]).then_inc(s_dve, 1)
                        chain[0] += 1
                        wait(dve, s_dve, base[0] + chain[0])
                        v.tensor_tensor(xT_lo[:], xT[:], xT_hi[:].bitcast(F32),
                                        ALU.subtract).then_inc(s_xT, 1)
                    elif kind in ("q", "k"):
                        qk = int(kind == "k")
                        wait(dve, s_part0, nxt * 2 + qk + 1)
                        v.scalar_tensor_tensor(out=rest[:, qk, :], in0=b[:],
                                               scalar=bqk[:, qk:qk + 1], in1=parts[:, 3 * qk, :],
                                               op0=ALU.add, op1=ALU.subtract).then_inc(s_vfree, 1)
                        wait(dve, s_vfree, unit + 1)
                        wait(dve, s_stack, nxt * 16 * STACK_DMAS)
                        v.tensor_copy(parts[:, 3 * qk + 1, :], rest[:, qk, :]).then_inc(s_dve, 1)
                        chain[0] += 1
                        wait(dve, s_dve, base[0] + chain[0])
                        v.tensor_tensor(parts[:, 3 * qk + 2, :], rest[:, qk, :],
                                        parts[:, 3 * qk + 1, :], ALU.subtract).then_inc(s_part, 1)
                    elif kind == "v":
                        wait(dve, s_pv, nxt * GROUPS)
                        if isinstance(i, int) and i < 0:
                            dve.wait_ge(s_const, 8)
                        v.tensor_tensor(v_sb[:, :, :, 0:HD],
                                        b[:].rearrange("p (t h d) -> p t h d", t=TB, d=HD),
                                        bv[:].rearrange("p (a h d) -> p a h d", a=1, d=HD)
                                        .broadcast_to([P, TB, HEADS, HD]),
                                        ALU.add).then_inc(s_vfree, 1)
                    elif kind == "smax":
                        _, grp, u = w
                        qb, heads = MAX_UNITS[u]
                        width = (qb + 1) * P
                        h0, h1 = heads[0], heads[-1]
                        dst = rowmax[:, grp, qb].rearrange("p r n -> p n r")[
                            :, h0 // 2:h1 // 2 + 1, h0 % 2:h1 % 2 + 1]
                        v.reduce_max(dst, b[:, 0:width * len(heads)]
                                     .rearrange("p (n r k) -> p n r k", k=width,
                                                n=h1 // 2 + 1 - h0 // 2),
                                     AX.X).then_inc(s_vfree, 1)
                        if u == NMAX - 1:
                            wait(dve, s_vfree, unit + 1)
                            m, r = rowmax[:, grp], nmr[:, grp]
                            part = [nm16[:, grp, :, :, k, :] for k in range(3)]
                            v.tensor_scalar(part[0], m, -1.0, None, ALU.mult).then_inc(s_dve, 1)
                            chain[0] += 1
                            wait(dve, s_dve, base[0] + chain[0])
                            v.scalar_tensor_tensor(out=r, in0=m, scalar=-1.0, in1=part[0],
                                                   op0=ALU.mult,
                                                   op1=ALU.subtract).then_inc(s_dve, 1)
                            chain[0] += 1
                            wait(dve, s_dve, base[0] + chain[0])
                            v.tensor_copy(part[1], r).then_inc(s_dve, 1)
                            chain[0] += 1
                            wait(dve, s_dve, base[0] + chain[0])
                            v.tensor_tensor(part[2], r, part[1], ALU.subtract).then_inc(s_nm, 1)
                    elif kind == "nm":
                        grp = w[1]
                        wait(dve, s_mrow[grp], i * 32)
                        v.tensor_copy(nmT[:, grp, :], b[:].bitcast(BF16)[0:12, 0:T])\
                            .then_inc(s_vfree, 1)
                    elif kind == "oT":
                        grp = w[1]
                        o = b[:].rearrange("p (t h d) -> p t h d", t=TB, h=GH)
                        v.reciprocal(rden[:, grp], o[:, :, :, HD]).then_inc(s_dve, 1)
                        chain[0] += 1
                        wait(dve, s_dve, base[0] + chain[0])
                        v.tensor_tensor(
                            o_tok[:, :, grp * GH * HD:(grp + 1) * GH * HD]
                            .rearrange("p t (h d) -> p t h d", h=GH),
                            o[:, :, :, 0:HD],
                            rden[:, grp].rearrange("p t (h a) -> p t h a", a=1)
                            .broadcast_to([P, TB, GH, HD]), ALU.mult).then_inc(s_vfree, 1)
                    elif kind == "OT":
                        v.tensor_copy(oT[:], b[:]).then_inc(s_vfree, 1)
                    elif kind == "proj":
                        wait(dve, s_xbp, i + 1)
                        wait(dve, s_x1old, i)
                        v.tensor_tensor(x1[:], b[:].rearrange("p (t c) -> p t c", t=TB), x_bp[:],
                                        ALU.add).then_inc(s_vfree, 1)
                    elif kind == "ln2":
                        wait(dve, s_vfree, first + units[("proj",)] + 1)
                        layernorm(x1, x2n, s_x2n)
                    elif kind == "x2T":
                        wait(dve, s_z, i * SLOTS)
                        v.tensor_copy(x2T[:], b[:]).then_inc(s_vfree, 1)
                        wait(dve, s_vfree, unit + 1)
                        v.tensor_copy(x2T_hi[:], x2T[:]).then_inc(s_dve, 1)
                        chain[0] += 1
                        wait(dve, s_dve, base[0] + chain[0])
                        v.tensor_tensor(x2T_lo[:], x2T[:], x2T_hi[:].bitcast(F32),
                                        ALU.subtract).then_inc(s_x2T, 1)
                    elif kind == "y" and w[1] % HC == HC - 1:
                        e = w[1] // HC
                        wait(dve, s_y, f * SLOTS + w[1] + 1)
                        if e in (0, 2):
                            wait(dve, s_wb[e // 2], f * 16 + 16)
                        wait(dve, s_acc, f * (EXPERTS - 1) + (max(e - 2, 1) if e > 1 else 0))
                        v.scalar_tensor_tensor(out=term[:, e % 2, :], in0=y_bank[:],
                                               scalar=b2_sb[:, e:e + 1], in1=wb[:, e, :],
                                               op0=ALU.add, op1=ALU.mult).then_inc(s_yfree, 1)
                    elif kind == "yT":
                        wait(dve, s_yT, f + 1)
                        wait(dve, s_x1old, f + 1)
                        wait(dve, s_out, f * 16)
                        v.tensor_tensor(o_sb[:], y_bank[:].rearrange("p (t c) -> p t c", t=TB),
                                        x1_old[:], ALU.add).then_inc(s_yfree, 1)
                if work is ORDER or work is FIRST:
                    assert chain[0] == CHAIN
                if work is FIRST_PREP:
                    assert chain[0] == CHAIN_PREP

            steps_over_sequences(dve, step)

        @block.tensor
        def _(pe):
            mm = nc.tensor.matmul

            def split_matmul(dst, hi, lo, x_hi, x_lo):
                mm(dst, hi, x_lo, start=True, stop=False)
                mm(dst, lo, x_hi, start=False, stop=False)
                return mm(dst, hi, x_hi, start=False, stop=True)

            def four_transposes(dst, src, identity):
                for t in range(TB):
                    last = nc.tensor.transpose(dst[:, t * P:(t + 1) * P], src(t), identity)
                return last

            pe.wait_ge(s_const, 11)
            pe.wait_ge(s_brow, 32)
            nc.tensor.transpose(y_bank[:, 0:NBR], b_rows[:], ident[0:NBR, 0:NBR]).then_inc(s_bT, 1)
            pe.wait_ge(s_vset, 10)

            def step(i, work):
                f, nxt, units, first = i - 1, i + 1, turn(work), v_count(i)
                for w in work:
                    kind = w[0]
                    if kind in V_KINDS:
                        unit = first + units[w]
                        b = v_bank[units[w] % 2]
                        wait(pe, s_vfree, first + max(units[w] - 1, 0))
                    if kind == "gate":
                        wait(pe, s_x2T, f + 1)
                        wait(pe, s_yfree, f * NY)
                        split_matmul(y_bank[:], wg_hi[:], wg_lo[:], x2T_hi[:],
                                     x2T_lo[:]).then_inc(s_gate, 1)
                    elif kind == "xT":
                        wait(pe, s_xn, nxt * TB + TB)
                        four_transposes(b, lambda t: xn[:, t, :], ident[:]).then_inc(s_vfull, 1)
                    elif kind in ("q", "k"):
                        qk = int(kind == "k")
                        wait(pe, s_xT, nxt + 1)
                        split_matmul(b[:], wqk_hi[:, qk, :], wqk_lo[:, qk, :], xT_hi[:],
                                     xT_lo[:]).then_inc(s_vfull, 1)
                    elif kind == "v":
                        for t in range(TB):
                            last = mm(b[:, t * P:(t + 1) * P], xT[:, t * P:(t + 1) * P],
                                      wqkv_in[:, 2 * C:], start=True, stop=True)
                        last.then_inc(s_vfull, 1)
                    elif kind == "smax":
                        _, grp, u = w
                        if grp == 0 and u == 0:
                            wait(pe, s_stack, (i + 1) * (16 * STACK_DMAS))
                        qb, heads = MAX_UNITS[u]
                        width = (qb + 1) * P
                        for n, j in enumerate(heads):
                            pair, row = (grp * GH + j) // 2, 64 * (j % 2)
                            rows = stack[row:row + 64, pair]
                            dst = b[:, n * width:(n + 1) * width]
                            mm(dst, rows[:, 0, qb * P:(qb + 1) * P], rows[:, 1, 0:width],
                               start=True, stop=False)
                            last = mm(dst[:, qb * P:], ident16[:], mask16[:], start=False,
                                      stop=True)
                        last.then_inc(s_vfull, 1)
                    elif kind == "nm":
                        grp = w[1]
                        wait(pe, s_nm, i * GROUPS + grp + 1)
                        b16 = b[:].bitcast(BF16)
                        four_transposes(b16[0:12, 0:T],
                                        lambda t: nm16[:, grp, t].rearrange("p r k n -> p (r k n)"),
                                        ident16[:]).then_inc(s_vfull, 1)
                    elif kind == "sexp":
                        _, grp, u = w
                        n = grp * NEXP + u
                        if u == 0:
                            wait(pe, s_mrow[grp], i * 32 + 32)
                        wait(pe, s_exp, i * GROUPS * NEXP + n - 1)
                        col = 0
                        for j, kb in EXP_UNITS[u]:
                            pair, row = (grp * GH + j) // 2, 64 * (j % 2)
                            rows = stack[row:row + 64, pair]
                            width = T - kb * P
                            last = mm(e_bank[n % 2][:, col:col + width],
                                      rows[:, 1, kb * P:(kb + 1) * P], rows[:, 0, kb * P:],
                                      start=True, stop=True)
                            col += width
                        last.then_inc(s_efull, 1)
                    elif kind == "pv":
                        grp = w[1]
                        wait(pe, s_mask, i * GROUPS * NEXP + (grp + 1) * NEXP)
                        wait(pe, s_og, i * GROUPS + grp)
                        for kb in range(TB):
                            for j in range(GH):
                                c = PT_COL[(j, kb)]
                                last = mm(pv_bank[32 * j:32 * j + 32, kb * P:],
                                          v_sb[:, kb, grp * GH + j, :],
                                          pt[:, grp % 2, c:c + T - kb * P], start=(kb == 0),
                                          stop=(kb == TB - 1))
                        last.then_inc(s_pv, 1)
                    elif kind == "oT":
                        grp = w[1]
                        wait(pe, s_og, i * GROUPS + grp + 1)
                        four_transposes(b, lambda t: o_grp[:, grp, t * P:(t + 1) * P],
                                        ident[:]).then_inc(s_vfull, 1)
                    elif kind == "OT":
                        wait(pe, s_vfree, unit)
                        four_transposes(b, lambda t: o_tok[:, t, :], ident[:]).then_inc(s_vfull, 1)
                    elif kind == "proj":
                        wait(pe, s_vfree, unit)
                        for t in range(TB):
                            last = mm(b[:, t * P:(t + 1) * P], oT[:, t * P:(t + 1) * P], wp[:],
                                      start=True, stop=True)
                        last.then_inc(s_vfull, 1)
                    elif kind == "x2T":
                        wait(pe, s_x2n, i * TB + TB)
                        four_transposes(b, lambda t: x2n[:, t, :], ident[:]).then_inc(s_vfull, 1)
                    elif kind == "z":
                        s = w[1]
                        if s == 0:
                            if not isinstance(i, int) or i == 1:
                                pe.wait_ge(s_w1lo, 1)
                        wait(pe, s_h, f * SLOTS + max(s - 1, 0))
                        split_matmul(z_bank[s % 2][:], w1_hi[:, s * P:(s + 1) * P],
                                     w1_lo[:, s * P:(s + 1) * P], x2T_hi[:],
                                     x2T_lo[:]).then_inc(s_z, 1)
                    elif kind == "y":
                        s = w[1]
                        wait(pe, s_h, f * SLOTS + s + 1)
                        if s == 0:
                            wait(pe, s_gtanh, f + 1)
                        elif s % HC == 0:
                            wait(pe, s_yfree, f * NY + s // HC)
                        mm(y_bank[:], w2_sb[:, s, :], hid[:, s % 2, :], start=(s % HC == 0),
                           stop=(s % HC == HC - 1)).then_inc(s_y, 1)
                    elif kind == "yT":
                        wait(pe, s_acc, f * (EXPERTS - 1) + EXPERTS - 1)
                        wait(pe, s_yfree, f * NY + EXPERTS)
                        four_transposes(y_bank, lambda t: acc[:, t * P:(t + 1) * P],
                                        ident[:]).then_inc(s_yT, 1)

            pe.wait_ge(s_w2, 16)
            steps_over_sequences(pe, step)




_INS = ["L0_attn_x", "L0_attn_w_qkv", "L0_attn_b_qkv", "L0_attn_w_proj", "L0_attn_b_proj",
        "L0_ffn_Wg", "L0_ffn_bg", "L0_ffn_W1", "L0_ffn_b1", "L0_ffn_W2", "L0_ffn_b2"]


def kernel(**inputs):
    import concourse.bacc as bacc
    from concourse.bass_utils import run_bass_kernel_spmd

    nc = bacc.Bacc("TRN2", target_bir_lowering=False, num_devices=1)
    arrays, args = {}, []
    for name in _INS:
        a = np.ascontiguousarray(inputs[name])
        arrays[f"in_{name}"] = a
        args.append(nc.dram_tensor(f"in_{name}", a.shape, mybir.dt.from_np(a.dtype),
                                   kind="ExternalInput").ap())
    out = nc.dram_tensor("out_x", (BATCH, T, C), F32, kind="ExternalOutput").ap()
    block_program(nc, *args, out)
    result = run_bass_kernel_spmd(nc, [arrays], core_ids=[0])
    return result.results[0]["out_x"]
```

```python
from contextlib import ExitStack

import numpy as np

import concourse.bass as bass
from concourse import mybir

F32 = mybir.dt.float32
F32R = mybir.dt.float32r
BF16 = mybir.dt.bfloat16
I32 = mybir.dt.int32
ALU = mybir.AluOpType
ACT = mybir.ActivationFunctionType
AX = mybir.AxisListType

BATCH, T, C = 8, 512, 128
HEADS, HD = 16, 8
EXPERTS, HIDDEN = 8, 512
P = 128
TB = T // P
HC = HIDDEN // P
SLOTS = EXPERTS * HC
PAIRS = HEADS // 2
GROUPS, GH = 4, 4
EPS = 1e-5
SCALE = float(HD) ** -0.5
MASKED = -1e38
RSQRT_SEED = 0x5F3759DF
NEWTON = 3

Q_PART = (0, 0, 1, 0, 1, 2)
K_PART = (0, 1, 0, 2, 1, 0)
M_SLOT = 6
STACK_DMAS = 7

MAX_UNITS = ([(3, (j,)) for j in range(GH)] + [(2, (j,)) for j in range(GH)]
             + [(qb, heads) for qb in (1, 0) for heads in ((0, 2), (1, 3))])
EXP_UNITS = []
for _a in (0, 1):
    for _j in (_a, _a + 2):
        EXP_UNITS += [((_j, 0),), ((_j, 1), (_j, 3))]
    EXP_UNITS += [((_a, 2), (_a + 2, 2))]
NMAX, NEXP = len(MAX_UNITS), len(EXP_UNITS)
PT_COL = {piece: u * T + sum((TB - q[1]) * P for q in unit[:n])
          for u, unit in enumerate(EXP_UNITS) for n, piece in enumerate(unit)}


SMAX_AT, SMAX_EVERY = 0.0, 1.052
SEXP_AT, SEXP_EVERY = 19.351, 1.28
EXPERTS_AT, EXPERTS_EVERY = 3.1, 0.85
LN1_AT, LN1_EVERY = 45, 0.513
LN2_AT, LN2_EVERY = 75.8, 0.35
AT = {"gate": 1.184, "xT": 54.713, "q": 57, "k": 57.13, "OT": 74.5, "v": 74.8, "proj": 75.5,
      "x2T": 86.679}
NM_AFTER, PV_AFTER, OT_AFTER = 2.0, 2.115, 2.435
LN_LINKS = 5 + 3 * NEWTON + 1


def order_of_work():
    plan = [(0, ("xbp",)), (0, ("xload",))] + [(t, (kind,)) for kind, t in AT.items()]
    plan += [(LN1_AT + k * LN1_EVERY, ("ln1", k)) for k in range(LN_LINKS)]
    plan += [(LN2_AT + k * LN2_EVERY, ("ln2", k)) for k in range(LN_LINKS)]
    for g in range(GROUPS):
        smax = [SMAX_AT + (g * NMAX + u) * SMAX_EVERY for u in range(NMAX)]
        sexp = [SEXP_AT + (g * NEXP + u) * SEXP_EVERY for u in range(NEXP)]
        plan += [(t, ("smax", g, u)) for u, t in enumerate(smax)]
        plan += [(smax[-1] + NM_AFTER, ("nm", g))]
        plan += [(t, ("sexp", g, u)) for u, t in enumerate(sexp)]
        plan += [(sexp[-1] + PV_AFTER, ("pv", g)), (sexp[-1] + PV_AFTER + OT_AFTER, ("oT", g))]
    plan += [(AT["OT"], ("stack",))]

    experts = [[("z", 0)]]
    for s in range(SLOTS):
        z = [[("z", s + 1), ("lo", s)] if s + 1 < SLOTS else [("lo", s)]]
        ylo = [[("ylo", s - 1)]] if s else []
        if s and s % HC == 0:
            ylo[0] += [("term", s // HC - 1)]
            experts += ylo + z
        else:
            experts += z + ylo
        experts += [[("yhi", s)]]
    experts += [[("ylo", SLOTS - 1), ("term", EXPERTS - 1)]]
    for n, steps in enumerate(experts):
        plan += [(EXPERTS_AT + n * EXPERTS_EVERY, step) for step in steps]

    plan.sort(key=lambda entry: entry[0])
    return [step for _, step in plan] + [("yT",), ("keep",)]


ORDER = order_of_work()
TAIL = sum(w[0] == "lo" for w in ORDER[:ORDER.index(("proj",))])
POOL_SPLITS = [s for s in range(SLOTS) if s >= TAIL or s % HC == 1]
VECTOR_SPLITS = [s for s in range(SLOTS) if s not in POOL_SPLITS]
EXPERT_KINDS = ("gate", "z", "lo", "yhi", "ylo", "term", "yT")
NEXT_KINDS = ("xload", "ln1", "xT", "q", "k", "v", "stack")
FIRST_PREP = [("ln1", k) for k in range(LN_LINKS)]
FIRST_PREP += [("weights",), ("xT",), ("q",), ("k",), ("v",), ("stack",), ("w1_hi",), ("w1_lo",)]
FIRST = [w for w in ORDER if w[0] not in EXPERT_KINDS]
FIRST = [v for w in FIRST
         for v in [w] + [("warm",)] * (w[0] in ("smax", "sexp"))]
FIRST = FIRST[:2] + [("w2_hi",), ("w2_lo",)] + [("warm",)] * 16 + FIRST[2:]
LAST = [w for w in ORDER if w[0] not in NEXT_KINDS]
EXPERT_WORK = [w for w in ORDER if w[0] in EXPERT_KINDS]
V_KINDS = ("xT", "q", "k", "v", "smax", "nm", "oT", "OT", "proj", "x2T")


def turn(work):
    return {w: n for n, w in enumerate(w for w in work if w[0] in V_KINDS)}


CHAIN_NORM = 2 * TB + 4 + 3 * NEWTON
CHAIN_PREP = CHAIN_NORM + 3
CHAIN = CHAIN_PREP + CHAIN_NORM + 1 + 3 * GROUPS + GROUPS
NV_PREP, NV = len(turn(FIRST_PREP)), len(turn(ORDER))
NY = EXPERTS + 1
WB = EXPERTS // 2
NBR = SLOTS + EXPERTS


def block_program(nc, x, w_qkv, b_qkv, w_proj, b_proj, w_gate, b_gate, w1, b1, w2, b2, out):
    gates_dram = nc.dram_tensor("gates", [EXPERTS, T], F32).ap()

    with ExitStack() as ctx:
        def sb(name, shape, dt=F32):
            return ctx.enter_context(nc.sbuf_tensor(name, shape, dt))

        def bank(name):
            return ctx.enter_context(nc.psum_tensor(name, [P, T], F32))

        def sem(name):
            return ctx.enter_context(nc.semaphore(name))

        ident = sb("ident", [P, P])
        ident16 = sb("ident16", [P, P], BF16)
        mask16 = sb("mask16", [P, P], BF16)
        wqkv_in = sb("wqkv_in", [P, 3 * C])
        wqk_hi = sb("wqk_hi", [P, 2, C], F32R)
        wqk_lo = sb("wqk_lo", [P, 2, C], F32R)
        bqk = sb("bqk", [P, 2])
        bv = sb("bv", [P, C])
        wp = sb("wp", [P, C])
        bp = sb("bp", [P, C])
        wg_in = sb("wg_in", [P, EXPERTS])
        wg_hi = sb("wg_hi", [P, P], F32R)
        wg_lo = sb("wg_lo", [P, P], F32R)
        bg_in = sb("bg_in", [EXPERTS, 1])
        hbg = sb("hbg", [EXPERTS, 1])
        w1_hi = sb("w1_hi", [P, EXPERTS * HIDDEN], F32R)
        w1_lo = sb("w1_lo", [P, EXPERTS * HIDDEN], F32R)
        w2_hi = sb("w2_hi", [P, SLOTS * C], F32R)
        w2_lo = sb("w2_lo", [P, SLOTS * C], F32R)
        b_rows = sb("b_rows", [NBR, P])
        b_cols = sb("b_cols", [P, NBR])
        b1_sb, b2_sb = b_cols[:, 0:SLOTS], b_cols[:, SLOTS:NBR]

        x_in = sb("x_in", [P, TB, C])
        x_bp = sb("x_bp", [P, TB, C])
        xn = sb("xn", [P, TB, C])
        stats = sb("stats", [P, TB, 6])
        mv = sb("mv", [P, TB, 2])
        var = sb("var", [P, TB])
        hvar = sb("hvar", [P, TB])
        seed = sb("seed", [P, TB], I32)
        rstd = sb("rstd", [P, NEWTON + 1, TB], I32)
        ysq = sb("ysq", [P, TB])
        yv = sb("yv", [P, TB])
        xT = sb("xT", [P, T])
        xT_hi = sb("xT_hi", [P, T], F32R)
        xT_lo = sb("xT_lo", [P, T], F32R)
        parts = sb("parts", [P, 6, T], BF16)
        stack = sb("stack", [P, PAIRS, 2, T], BF16)
        v_sb = sb("v_sb", [P, TB, HEADS, 32])
        rowmax = sb("rowmax", [P, GROUPS, TB, 2, 2])
        nm16 = sb("nm16", [P, GROUPS, TB, 2, 3, 2], BF16)
        nmr = sb("nmr", [P, GROUPS, TB, 2, 2])
        nmT = sb("nmT", [12, 2, T], BF16)
        pt = sb("pt", [P, 2, NEXP * T])
        w1_in, w2_in = pt[:, 0, 0:EXPERTS * HIDDEN], pt[:, 1, 0:SLOTS * C]
        o_grp = sb("o_grp", [P, 2, T])
        rden = sb("rden", [P, GROUPS, TB, GH])
        o_tok = sb("o_tok", [P, TB, C])
        oT = sb("oT", [P, T])
        rest = oT
        x1 = sb("x1", [P, TB, C])

        x2n = xn
        x2T_hi = sb("x2T_hi", [P, T], F32R)
        x2T_lo = sb("x2T_lo", [P, T], F32R)
        x1_old = sb("x1_old", [P, TB, C])
        g_tanh = sb("g_tanh", [EXPERTS, T])
        g_prob = sb("g_prob", [EXPERTS, T])
        g_w = sb("g_w", [EXPERTS, T])
        wb = sb("wb", [P, WB, T])
        h_hi = sb("h_hi", [P, 2, T], F32R)
        h_all = sb("h_all", [P, 2, T])
        h_lo = sb("h_lo", [P, 2, T], F32R)
        term = sb("term", [P, 2, T])
        acc = sb("acc", [P, T])
        o_sb = sb("o_sb", [P, TB, C])

        v_bank = [bank("v_bank0"), bank("v_bank1")]
        e_bank = [bank("e_bank0"), bank("e_bank1")]
        pv_bank = bank("pv_bank")
        z_bank = [bank("z_bank0"), bank("z_bank1")]
        y_bank = bank("y_bank")

        s_wqkv = sem("s_wqkv")
        s_wgt = sem("s_wgt")
        s_w1 = sem("s_w1")
        s_w2 = sem("s_w2")
        s_brow = sem("s_brow")
        s_bT = sem("s_bT")
        s_const = sem("s_const")
        s_vset = sem("s_vset")
        s_whi = sem("s_whi")
        s_wlo = sem("s_wlo")
        s_x = sem("s_x")
        s_xbp = sem("s_xbp")
        s_dve = sem("s_dve")
        s_xn = sem("s_xn")
        s_xT = sem("s_xT")
        s_part0 = sem("s_part0")
        s_part = sem("s_part")
        s_stack = sem("s_stack")
        s_vfull = sem("s_vfull")
        s_vfree = sem("s_vfree")
        s_nm = sem("s_nm")
        s_mrow = [sem(f"s_mrow{g}") for g in range(GROUPS)]
        s_efull = sem("s_efull")
        s_exp = sem("s_exp")
        s_mask = sem("s_mask")
        s_pv = sem("s_pv")
        s_og = sem("s_og")
        s_x2n = sem("s_x2n")
        s_x1old = sem("s_x1old")
        s_gate = sem("s_gate")
        s_gtanh = sem("s_gtanh")
        s_gprob = sem("s_gprob")
        s_gw = sem("s_gw")
        s_gout = sem("s_gout")
        s_wb = sem("s_wb")
        s_z = sem("s_z")
        s_hhi = sem("s_hhi")
        s_hall = sem("s_hall")
        s_hlo = sem("s_hlo")
        s_hlo_pool = sem("s_hlo_pool")
        s_yhi = sem("s_yhi")
        s_ylo = sem("s_ylo")
        s_yfree = sem("s_yfree")
        s_acc = sem("s_acc")
        s_yT = sem("s_yT")
        s_out = sem("s_out")

        s_apart = {}

        primed = (s_hhi, s_hall, s_hlo, s_hlo_pool, s_yhi, s_ylo, s_yfree, s_gw, s_gout, s_acc,
                  s_yT, s_out)

        def wait(eng, s, n):
            if not isinstance(n, int) or n > 0:
                eng.wait_ge(s, n + 1 if s in primed else n)

        def wait_apart(eng, s, n):
            if not isinstance(n, int) or n > 0:
                wait(eng, s, n)
                if not isinstance(n, int):
                    eng.sem_inc(s_apart[id(eng)], 1)

        def split_done(eng, f, s):
            if s in VECTOR_SPLITS:
                wait(eng, s_hlo, f * len(VECTOR_SPLITS) + VECTOR_SPLITS.index(s) + 1)
            else:
                wait(eng, s_hlo_pool, f * len(POOL_SPLITS) + POOL_SPLITS.index(s) + 1)

        x_v = x.rearrange("b (t p) c -> b p t c", p=P)
        out_v = out.rearrange("b (t p) c -> b p t c", p=P)
        block = ctx.enter_context(nc.Block())

        def steps_over_sequences(eng, step):
            step(-1, FIRST_PREP)
            step(0, FIRST)
            with eng.Fori(1, BATCH - 1) as i:
                step(i, ORDER)
            step(BATCH - 1, LAST)
            step(BATCH, EXPERT_WORK)

        def v_count(i):
            if isinstance(i, int) and i in (-1, BATCH):
                return 0 if i < 0 else NV_PREP + (BATCH - 1) * NV + len(turn(LAST))
            return NV_PREP + i * NV

        @block.sync
        def _(sp):
            s_apart[id(sp)] = sem("s_apart_sp")
            for s in primed:
                sp.sem_inc(s, 1)
            sp.dma_start(x_in[:], x_v[0]).then_inc(s_x, 16)
            sp.dma_start(wqkv_in[:], w_qkv).then_inc(s_wqkv, 16)
            for qk in range(2):
                src = b_qkv[qk * C:(qk + 1) * C].rearrange("(n r) -> r n", n=PAIRS)
                sp.dma_start(bqk[:, qk:qk + 1], src,
                             allow_slow_non_contiguous=True).then_inc(s_wqkv, 16)
            sp.dma_start(bv[:], b_qkv[2 * C:].rearrange("(a c) -> a c", a=1)
                         .broadcast_to([P, C])).then_inc(s_wqkv, 16)
            sp.dma_start(bp[:], b_proj.rearrange("(a c) -> a c", a=1)
                         .broadcast_to([P, C])).then_inc(s_wqkv, 16)
            sp.dma_start(wp[:], w_proj).then_inc(s_wqkv, 16)
            sp.dma_start(wg_in[:], w_gate).then_inc(s_wgt, 16)
            sp.dma_start(bg_in[:], b_gate.rearrange("(e a) -> e a", a=1),
                         allow_slow_non_contiguous=True).then_inc(s_wgt, 16)
            sp.dma_start(b_rows[0:SLOTS, :],
                         b1.rearrange("e (c p) -> (e c) p", p=P)).then_inc(s_brow, 16)
            sp.dma_start(b_rows[SLOTS:NBR, :], b2).then_inc(s_brow, 16)
            sp.dma_start(w1_in.rearrange("p (e h) -> p e h", e=EXPERTS),
                         w1.rearrange("e d h -> d e h")).then_inc(s_w1, 16)

            def step(i, work):
                f, nxt, unit, first = i - 1, i + 1, turn(work), v_count(i)
                for w in work:
                    if w[0] == "gate":
                        wait_apart(sp, s_gw, f + 1)
                        sp.dma_start(gates_dram, g_w[:]).then_inc(s_gout, 16)
                        wait_apart(sp, s_gout, f * 16 + 16)
                        wait_apart(sp, s_yfree, f * NY)
                        sp.dma_start(wb[:], gates_dram[0:WB].rearrange("(a e) t -> a e t", a=1)
                                     .broadcast_to([P, WB, T])).then_inc(s_wb, 16)
                    elif w == ("term", WB - 1):
                        wait_apart(sp, s_yfree, f * NY + WB)
                        sp.dma_start(wb[:], gates_dram[WB:].rearrange("(a e) t -> a e t", a=1)
                                     .broadcast_to([P, WB, T])).then_inc(s_wb, 16)
                    elif w[0] == "stack":
                        wait_apart(sp, s_part, nxt * 2 + 2)
                        wait_apart(sp, s_efull, nxt * GROUPS * NEXP)
                        if isinstance(i, int) and i < 0:
                            sp.wait_ge(s_const, 10)
                        for s, (a, b) in enumerate(zip(Q_PART, K_PART)):
                            src = parts[:, a:4 + b:3 + b - a, :]
                            sp.dma_start(stack[s::8, :, :, :], src).then_inc(s_stack, 16)
                        sp.dma_start(stack[M_SLOT::8, :, 0, :],
                                     stack[M_SLOT + 1::8, :, 0, :]).then_inc(s_stack, 16)
                    elif w[0] == "w2_hi":
                        sp.dma_start(w2_in.rearrange("p (s d) -> p s d", s=SLOTS),
                                     w2.rearrange("e (c p) d -> p (e c) d", p=P)).then_inc(s_w2, 16)
                    elif w[0] == "nm":
                        g = w[1]
                        wait_apart(sp, s_vfree, first + unit[w] + 1)
                        for par in range(2):
                            r = 64 * par + M_SLOT
                            sp.dma_start(stack[r:r + 17:8, 2 * g:2 * g + 2, 0, :],
                                         nmT[6 * par:6 * par + 6, g % 2, :]).then_inc(s_mrow[g], 16)
                    elif w[0] == "xload":
                        wait_apart(sp, s_xn, i * TB + TB)
                        wait_apart(sp, s_xbp, i + 1)
                        src = x_v[nxt] if isinstance(nxt, int) else \
                            x_v[bass.ds(nxt, 1)].rearrange("a p t c -> (a p) t c")
                        sp.dma_start(x_in[:], src).then_inc(s_x, 16)
                    elif w[0] == "yT":
                        wait_apart(sp, s_yfree, f * NY + NY)
                        dst = out_v[f] if isinstance(f, int) else \
                            out_v[bass.ds(f, 1)].rearrange("a p t c -> (a p) t c")
                        sp.dma_start(dst, o_sb[:]).then_inc(s_out, 16)

            steps_over_sequences(sp, step)
            wait(sp, s_out, 16 * BATCH)

        @block.gpsimd
        def _(pool):
            s_apart[id(pool)] = sem("s_apart_pool")
            g = nc.gpsimd
            g.memset(ident[:], 0.0).then_inc(s_const, 1)
            g.memset(ident16[:], 0.0).then_inc(s_const, 1)
            g.memset(mask16[:], 0.0).then_inc(s_const, 1)
            pool.wait_ge(s_const, 3)
            for m in (ident, ident16):
                g.affine_select(out=m[:], in_=m[:], compare_op=ALU.not_equal, fill=1.0, base=0,
                                pattern=[[-1, P]], channel_multiplier=1).then_inc(s_const, 1)
            g.affine_select(out=mask16[:], in_=mask16[:], compare_op=ALU.is_ge, fill=MASKED,
                            base=0, pattern=[[-1, P]], channel_multiplier=1).then_inc(s_const, 1)
            g.memset(stack[:, :, 0, :], 0.0).then_inc(s_const, 1)
            g.memset(stack[:, :, 1, :], 1.0).then_inc(s_const, 1)
            g.memset(v_sb[:], 0.0).then_inc(s_const, 1)
            pool.wait_ge(s_const, 9)
            g.memset(v_sb[:, :, :, HD:HD + 1], 1.0).then_inc(s_const, 1)

            def step(i, work):
                f = i - 1
                for w in work:
                    if w[0] == "w1_lo":
                        pool.wait_ge(s_whi, 1)
                        g.tensor_tensor(w1_lo[:], w1_in, w1_hi[:].bitcast(F32),
                                        ALU.subtract).then_inc(s_wlo, 1)
                    elif w[0] == "w2_lo":
                        pool.wait_ge(s_whi, 2)
                        g.tensor_tensor(w2_lo[:], w2_in, w2_hi[:].bitcast(F32),
                                        ALU.subtract).then_inc(s_wlo, 1)
                    elif w[0] == "xbp":
                        wait(pool, s_x, i * 16 + 16)
                        if isinstance(i, int) and i == 0:
                            pool.wait_ge(s_wqkv, 6 * 16)
                        wait(pool, s_vfree, v_count(i))
                        g.tensor_tensor(x_bp[:], x_in[:],
                                        bp[:].rearrange("p (a c) -> p a c", a=1)
                                        .broadcast_to([P, TB, C]), ALU.add).then_inc(s_xbp, 1)
                    elif w[0] == "sexp":
                        _, grp, u = w
                        n = grp * NEXP + u
                        wait_apart(pool, s_exp, i * GROUPS * NEXP + n + 1)
                        cols = [PT_COL[piece] for piece in EXP_UNITS[u]]
                        step_ = cols[1] - cols[0] if len(cols) > 1 else P
                        a = pt[:, grp % 2, cols[0]:cols[0] + step_ * (len(cols) - 1) + P]
                        if len(cols) > 1:
                            a = pt[:, grp % 2, u * T:(u + 1) * T]
                            if step_ == 2 * P:
                                a = a.rearrange("p (a c) -> p a c", a=2)[:, :, 0:P]
                            else:
                                a = a.rearrange("p (a c) -> p a c", a=4)[:, 0::3, :]
                        else:
                            a = a.rearrange("p (a c) -> p a c", a=1)
                        g.affine_select(out=a, in_=a, compare_op=ALU.is_ge, fill=0.0, base=0,
                                        pattern=[[0, len(cols)], [1, P]],
                                        channel_multiplier=-1).then_inc(s_mask, 1)
                    elif w[0] == "lo" and w[1] in POOL_SPLITS:
                        s = w[1]
                        wait(pool, s_hall, f * SLOTS + s + 1)
                        wait(pool, s_ylo, f * SLOTS + max(s - 1, 0))
                        g.tensor_tensor(h_lo[:, s % 2, :], h_all[:, s % 2, :],
                                        h_hi[:, s % 2, :].bitcast(F32),
                                        ALU.subtract).then_inc(s_hlo_pool, 1)
                    elif w[0] == "term" and w[1] >= 1:
                        e = w[1]
                        wait(pool, s_yfree, f * NY + 1 + e)
                        if e > 1:
                            wait(pool, s_acc, f * (EXPERTS - 1) + e - 1)
                        else:
                            wait(pool, s_yT, f)
                        g.tensor_tensor(acc[:], term[:, 0, :] if e == 1 else acc[:],
                                        term[:, e % 2, :], ALU.add).then_inc(s_acc, 1)

            steps_over_sequences(pool, step)

        @block.scalar
        def _(act):
            sc = nc.scalar
            def step(i, work):
                f, nxt, unit, first = i - 1, i + 1, turn(work), v_count(i)
                for w in work:
                    kind = w[0]
                    if kind == "w1_hi":
                        act.wait_ge(s_w1, 16)
                        sc.activation(w1_hi[:], w1_in, ACT.Copy).then_inc(s_whi, 1)
                    elif kind == "w2_hi":
                        act.wait_ge(s_w2, 16)
                        sc.activation(w2_hi[:], w2_in, ACT.Copy).then_inc(s_whi, 1)
                    elif kind == "gate":
                        wait(act, s_gate, f + 1)
                        wait(act, s_gw, f)
                        sc.activation(g_tanh[:], z_bank[1][0:EXPERTS, :], ACT.Tanh, scale=0.5,
                                      bias=hbg[:]).then_inc(s_gtanh, 1)
                    elif kind in ("q", "k"):
                        qk = int(kind == "k")
                        wait(act, s_vfull, first + unit[w] + 1)
                        wait(act, s_stack, nxt * 16 * STACK_DMAS)
                        sc.activation(parts[:, 3 * qk, :], v_bank[unit[w] % 2][:], ACT.Identity,
                                      bias=bqk[:, qk:qk + 1]).then_inc(s_part0, 1)
                    elif kind == "z":
                        s = w[1]
                        wait(act, s_z, f * SLOTS + s + 1)
                        wait(act, s_yhi, f * SLOTS + max(s - 1, 0))
                        if s >= 2:
                            split_done(act, f, s - 2)
                        sc.activation(h_hi[:, s % 2, :], z_bank[s % 2][:], ACT.Relu,
                                      bias=b1_sb[:, s:s + 1]).then_inc(s_hhi, 1)
                        sc.activation(h_all[:, s % 2, :], z_bank[s % 2][:], ACT.Relu,
                                      bias=b1_sb[:, s:s + 1]).then_inc(s_hall, 1)
                    elif kind == "sexp":
                        _, grp, u = w
                        n = grp * NEXP + u
                        wait(act, s_efull, i * GROUPS * NEXP + n + 1)
                        if u == 0:
                            wait(act, s_pv, i * GROUPS + grp - 1 if grp else i * GROUPS)
                            if isinstance(i, int) and i == 0 and grp < 2:
                                act.wait_ge(s_wlo, grp + 1)
                        sc.activation(pt[:, grp % 2, u * T:(u + 1) * T], e_bank[n % 2][:],
                                      ACT.Exp, scale=SCALE).then_inc(s_exp, 1)
                    elif kind == "pv":
                        grp = w[1]
                        wait(act, s_pv, i * GROUPS + grp + 1)
                        if grp > 1:
                            wait(act, s_vfull, first + unit[("oT", grp - 2)] + 1)
                        sc.activation(o_grp[:, grp % 2, :], pv_bank[:], ACT.Copy).then_inc(s_og, 1)
                    elif kind == "keep":
                        wait(act, s_vfree, first + unit[("proj",)] + 1)
                        wait(act, s_yfree, i * NY)
                        sc.activation(x1_old[:], x1[:], ACT.Copy).then_inc(s_x1old, 1)

            steps_over_sequences(act, step)

        @block.vector
        def _(dve):
            s_apart[id(dve)] = sem("s_apart_dve")
            v = nc.vector
            def norm_link(k, src, dst, done):
                def chained(ins):
                    ins.then_inc(s_dve, 1)
                    chain[0] += 1

                if k:
                    (wait_apart if k == 1 else wait)(dve, s_dve, base[0] + chain[0])
                n, part = divmod(k - 5, 3)
                if k == 0:
                    for t in range(TB):
                        chained(v.bn_stats(stats[:, t, :], src[:, t, :]))
                elif k == 1:
                    for t in range(TB):
                        chained(v.bn_aggr(mv[:, t, :], stats[:, t, :]))
                elif k == 2:
                    chained(v.tensor_scalar(var[:], mv[:, :, 1], EPS, None, ALU.add))
                    chained(v.tensor_scalar(hvar[:], mv[:, :, 1], EPS, 0.5, ALU.add, ALU.mult))
                elif k == 3:
                    chained(v.tensor_scalar(seed[:], var[:].bitcast(I32), 1, None,
                                            ALU.logical_shift_right))
                elif k == 4:
                    chained(v.tensor_scalar(rstd[:, 0, :], seed[:], -1, RSQRT_SEED - 2 ** 31,
                                            ALU.mult, ALU.add))
                elif n == NEWTON:
                    for t in range(TB):
                        v.tensor_scalar(dst[:, t, :], src[:, t, :], mv[:, t, 0:1],
                                        rstd[:, NEWTON, t:t + 1].bitcast(F32), ALU.subtract,
                                        ALU.mult).then_inc(done, 1)
                elif part == 0:
                    y = rstd[:, n, :].bitcast(F32)
                    chained(v.tensor_tensor(ysq[:], y, y, ALU.mult))
                elif part == 1:
                    chained(v.tensor_tensor(yv[:], ysq[:], hvar[:], ALU.mult))
                else:
                    chained(v.scalar_tensor_tensor(out=rstd[:, n + 1, :].bitcast(F32), in0=yv[:],
                                                   scalar=1.5, in1=rstd[:, n, :].bitcast(F32),
                                                   op0=ALU.subtract, op1=ALU.mult))

            chain, base = [0], [0]
            def prepare_weights():
                dve.wait_ge(s_wqkv, 6 * 16)
                for qk in range(2):
                    src = wqkv_in[:, qk * C:(qk + 1) * C].rearrange("p (n r) -> p r n", n=PAIRS)
                    hi = wqk_hi[:, qk, :].rearrange("p (r n) -> p r n", n=PAIRS)
                    v.tensor_copy(hi, src).then_inc(s_vset, 1)
                    dve.wait_ge(s_vset, 2 * qk + 1)
                    v.tensor_tensor(wqk_lo[:, qk, :].rearrange("p (r n) -> p r n", n=PAIRS), src,
                                    hi.bitcast(F32), ALU.subtract).then_inc(s_vset, 1)
                v.memset(wg_hi[:].bitcast(F32), 0.0).then_inc(s_vset, 1)
                v.memset(wg_lo[:].bitcast(F32), 0.0).then_inc(s_vset, 1)
                dve.wait_ge(s_wgt, 32)
                dve.wait_ge(s_vset, 6)
                v.tensor_copy(wg_hi[:, 0:EXPERTS], wg_in[:]).then_inc(s_vset, 1)
                v.tensor_scalar(hbg[:], bg_in[:], 0.5, None, ALU.mult).then_inc(s_vset, 1)
                dve.wait_ge(s_vset, 8)
                v.tensor_tensor(wg_lo[:, 0:EXPERTS], wg_in[:], wg_hi[:, 0:EXPERTS].bitcast(F32),
                                ALU.subtract).then_inc(s_vset, 1)
                dve.wait_ge(s_bT, 1)
                v.tensor_copy(b_cols[:], y_bank[:, 0:NBR]).then_inc(s_vset, 1)

            def step(i, work):
                f, nxt, units, first = i - 1, i + 1, turn(work), v_count(i)
                chain[0] = 0
                base[0] = 0 if isinstance(i, int) and i < 0 else CHAIN_PREP + i * CHAIN
                for w in work:
                    kind = w[0]
                    if kind in V_KINDS:
                        unit = first + units[w]
                        b = v_bank[units[w] % 2]
                        if kind not in ("q", "k"):
                            wait(dve, s_vfull, unit + 1)
                    if kind == "weights":
                        prepare_weights()
                    elif kind == "gate":
                        wait(dve, s_gtanh, f + 1)
                        v.tensor_scalar(g_prob[:], g_tanh[:], 0.5, 0.5, ALU.mult,
                                        ALU.add).then_inc(s_gprob, 1)
                        wait(dve, s_gprob, f + 1)
                        wait(dve, s_gout, f * 16)
                        v.scalar_tensor_tensor(out=g_w[:], in0=g_tanh[:], scalar=0.0,
                                               in1=g_prob[:], op0=ALU.is_gt,
                                               op1=ALU.mult).then_inc(s_gw, 1)
                    elif kind == "ln1":
                        if w[1] == 0:
                            wait(dve, s_x, nxt * 16 + 16)
                        norm_link(w[1], x_in, xn, s_xn)
                    elif kind == "xT":
                        v.tensor_copy(xT[:], b[:]).then_inc(s_vfree, 1)
                        wait(dve, s_vfree, unit + 1)
                        v.tensor_copy(xT_hi[:], xT[:]).then_inc(s_dve, 1)
                        chain[0] += 1
                        wait(dve, s_dve, base[0] + chain[0])
                        v.tensor_tensor(xT_lo[:], xT[:], xT_hi[:].bitcast(F32),
                                        ALU.subtract).then_inc(s_xT, 1)
                    elif kind in ("q", "k"):
                        qk = int(kind == "k")
                        wait(dve, s_part0, nxt * 2 + qk + 1)
                        wait(dve, s_part, nxt * 2 + qk)
                        v.scalar_tensor_tensor(out=rest[:], in0=b[:],
                                               scalar=bqk[:, qk:qk + 1], in1=parts[:, 3 * qk, :],
                                               op0=ALU.add, op1=ALU.subtract).then_inc(s_vfree, 1)
                        wait(dve, s_vfree, unit + 1)
                        wait(dve, s_stack, nxt * 16 * STACK_DMAS)
                        v.tensor_copy(parts[:, 3 * qk + 1, :], rest[:]).then_inc(s_dve, 1)
                        chain[0] += 1
                        wait(dve, s_dve, base[0] + chain[0])
                        v.tensor_tensor(parts[:, 3 * qk + 2, :], rest[:],
                                        parts[:, 3 * qk + 1, :], ALU.subtract).then_inc(s_part, 1)
                    elif kind == "v":
                        wait(dve, s_pv, nxt * GROUPS)
                        if isinstance(i, int) and i < 0:
                            dve.wait_ge(s_const, 10)
                        v.tensor_tensor(v_sb[:, :, :, 0:HD],
                                        b[:].rearrange("p (t h d) -> p t h d", t=TB, d=HD),
                                        bv[:].rearrange("p (a h d) -> p a h d", a=1, d=HD)
                                        .broadcast_to([P, TB, HEADS, HD]),
                                        ALU.add).then_inc(s_vfree, 1)
                    elif kind == "smax":
                        _, grp, u = w
                        qb, heads = MAX_UNITS[u]
                        width = (qb + 1) * P
                        h0, h1 = heads[0], heads[-1]
                        dst = rowmax[:, grp, qb].rearrange("p r n -> p n r")[
                            :, h0 // 2:h1 // 2 + 1, h0 % 2:h1 % 2 + 1]
                        v.reduce_max(dst, b[:, 0:width * len(heads)]
                                     .rearrange("p (n r k) -> p n r k", k=width,
                                                n=h1 // 2 + 1 - h0 // 2),
                                     AX.X).then_inc(s_vfree, 1)
                        if u == NMAX - 1:
                            wait(dve, s_vfree, unit + 1)
                            m, r = rowmax[:, grp], nmr[:, grp]
                            part = [nm16[:, grp, :, :, k, :] for k in range(3)]
                            v.tensor_scalar(part[0], m, -1.0, None, ALU.mult).then_inc(s_dve, 1)
                            chain[0] += 1
                            wait(dve, s_dve, base[0] + chain[0])
                            v.scalar_tensor_tensor(out=r, in0=m, scalar=-1.0, in1=part[0],
                                                   op0=ALU.mult,
                                                   op1=ALU.subtract).then_inc(s_dve, 1)
                            chain[0] += 1
                            wait(dve, s_dve, base[0] + chain[0])
                            v.tensor_copy(part[1], r).then_inc(s_dve, 1)
                            chain[0] += 1
                            wait(dve, s_dve, base[0] + chain[0])
                            v.tensor_tensor(part[2], r, part[1], ALU.subtract).then_inc(s_nm, 1)
                    elif kind == "nm":
                        grp = w[1]
                        wait(dve, s_mrow[(grp + 2) % GROUPS], i * 32 + (32 if grp > 1 else 0))
                        v.tensor_copy(nmT[:, grp % 2, :], b[:].bitcast(BF16)[0:12, 0:T])\
                            .then_inc(s_vfree, 1)
                    elif kind == "oT":
                        grp = w[1]
                        o = b[:].rearrange("p (t h d) -> p t h d", t=TB, h=GH)
                        v.reciprocal(rden[:, grp], o[:, :, :, HD]).then_inc(s_dve, 1)
                        chain[0] += 1
                        wait(dve, s_dve, base[0] + chain[0])
                        v.tensor_tensor(
                            o_tok[:, :, grp * GH * HD:(grp + 1) * GH * HD]
                            .rearrange("p t (h d) -> p t h d", h=GH),
                            o[:, :, :, 0:HD],
                            rden[:, grp].rearrange("p t (h a) -> p t h a", a=1)
                            .broadcast_to([P, TB, GH, HD]), ALU.mult).then_inc(s_vfree, 1)
                    elif kind == "OT":
                        v.tensor_copy(oT[:], b[:]).then_inc(s_vfree, 1)
                    elif kind == "proj":
                        wait(dve, s_xbp, i + 1)
                        wait(dve, s_x1old, i)
                        v.tensor_tensor(x1[:], b[:].rearrange("p (t c) -> p t c", t=TB), x_bp[:],
                                        ALU.add).then_inc(s_vfree, 1)
                    elif kind == "ln2":
                        if w[1] == 0:
                            wait(dve, s_vfree, first + units[("proj",)] + 1)
                        norm_link(w[1], x1, x2n, s_x2n)
                    elif kind == "x2T":
                        wait(dve, s_z, i * SLOTS)
                        v.tensor_copy(x2T_hi[:], b[:]).then_inc(s_dve, 1)
                        chain[0] += 1
                        wait(dve, s_dve, base[0] + chain[0])
                        v.tensor_tensor(x2T_lo[:], b[:], x2T_hi[:].bitcast(F32),
                                        ALU.subtract).then_inc(s_vfree, 1)
                    elif kind == "lo" and w[1] in VECTOR_SPLITS:
                        s = w[1]
                        wait(dve, s_hall, f * SLOTS + s + 1)
                        wait(dve, s_ylo, f * SLOTS + max(s - 1, 0))
                        v.tensor_tensor(h_lo[:, s % 2, :], h_all[:, s % 2, :],
                                        h_hi[:, s % 2, :].bitcast(F32),
                                        ALU.subtract).then_inc(s_hlo, 1)
                    elif kind == "term":
                        e = w[1]
                        wait(dve, s_ylo, f * SLOTS + (e + 1) * HC)
                        if e % WB == 0:
                            wait(dve, s_wb, f * 32 + 16 * (e // WB + 1))
                        wait(dve, s_acc, f * (EXPERTS - 1) + (max(e - 2, 1) if e > 1 else 0))
                        v.scalar_tensor_tensor(out=term[:, e % 2, :], in0=y_bank[:],
                                               scalar=b2_sb[:, e:e + 1], in1=wb[:, e % WB, :],
                                               op0=ALU.add, op1=ALU.mult).then_inc(s_yfree, 1)
                    elif kind == "yT":
                        wait(dve, s_yT, f + 1)
                        wait(dve, s_x1old, f + 1)
                        wait(dve, s_out, f * 16)
                        v.tensor_tensor(o_sb[:], y_bank[:].rearrange("p (t c) -> p t c", t=TB),
                                        x1_old[:], ALU.add).then_inc(s_yfree, 1)
                if work is ORDER or work is FIRST:
                    assert chain[0] == CHAIN
                if work is FIRST_PREP:
                    assert chain[0] == CHAIN_PREP

            steps_over_sequences(dve, step)

        @block.tensor
        def _(pe):
            mm = nc.tensor.matmul

            def split_matmul(dst, hi, lo, x_hi, x_lo):
                mm(dst, hi, x_lo, start=True, stop=False)
                mm(dst, lo, x_hi, start=False, stop=False)
                return mm(dst, hi, x_hi, start=False, stop=True)

            def four_transposes(dst, src, identity):
                for t in range(TB):
                    last = nc.tensor.transpose(dst[:, t * P:(t + 1) * P], src(t), identity)
                return last

            def step(i, work):
                f, nxt, units, first = i - 1, i + 1, turn(work), v_count(i)
                for w in work:
                    kind = w[0]
                    if kind in V_KINDS:
                        unit = first + units[w]
                        b = v_bank[units[w] % 2]
                        wait(pe, s_vfree, first + max(units[w] - 1, 0))
                    if kind == "weights":
                        pe.wait_ge(s_const, 6)
                        pe.wait_ge(s_brow, 32)
                        nc.tensor.transpose(y_bank[:, 0:NBR], b_rows[:],
                                            ident[0:NBR, 0:NBR]).then_inc(s_bT, 1)
                    elif kind == "warm":
                        pe.wait_ge(s_whi, 1)
                        mm(z_bank[0][:], w1_hi[:, 0:P], w1_hi[:, 0:T], start=True, stop=True)
                    elif kind == "gate":
                        wait(pe, s_vfree, first)
                        wait(pe, s_hall, f * SLOTS)
                        split_matmul(z_bank[1][:], wg_hi[:], wg_lo[:], x2T_hi[:],
                                     x2T_lo[:]).then_inc(s_gate, 1)
                    elif kind == "xT":
                        wait(pe, s_xn, nxt * TB + TB)
                        four_transposes(b, lambda t: xn[:, t, :], ident[:]).then_inc(s_vfull, 1)
                    elif kind in ("q", "k"):
                        qk = int(kind == "k")
                        wait(pe, s_xT, nxt + 1)
                        if work is FIRST_PREP:
                            pe.wait_ge(s_vset, 10)
                        split_matmul(b[:], wqk_hi[:, qk, :], wqk_lo[:, qk, :], xT_hi[:],
                                     xT_lo[:]).then_inc(s_vfull, 1)
                    elif kind == "v":
                        for t in range(TB):
                            last = mm(b[:, t * P:(t + 1) * P], xT[:, t * P:(t + 1) * P],
                                      wqkv_in[:, 2 * C:], start=True, stop=True)
                        last.then_inc(s_vfull, 1)
                    elif kind == "smax":
                        _, grp, u = w
                        if grp == 0 and u == 0:
                            wait(pe, s_stack, (i + 1) * (16 * STACK_DMAS))
                        qb, heads = MAX_UNITS[u]
                        width = (qb + 1) * P
                        for n, j in enumerate(heads):
                            pair, row = (grp * GH + j) // 2, 64 * (j % 2)
                            rows = stack[row:row + 64, pair]
                            dst = b[:, n * width:(n + 1) * width]
                            mm(dst, rows[:, 0, qb * P:(qb + 1) * P], rows[:, 1, 0:width],
                               start=True, stop=False)
                            last = mm(dst[:, qb * P:], ident16[:], mask16[:], start=False,
                                      stop=True)
                        last.then_inc(s_vfull, 1)
                    elif kind == "nm":
                        grp = w[1]
                        wait(pe, s_nm, i * GROUPS + grp + 1)
                        b16 = b[:].bitcast(BF16)
                        four_transposes(b16[0:12, 0:T],
                                        lambda t: nm16[:, grp, t].rearrange("p r k n -> p (r k n)"),
                                        ident16[:]).then_inc(s_vfull, 1)
                    elif kind == "sexp":
                        _, grp, u = w
                        n = grp * NEXP + u
                        if u == 0:
                            wait(pe, s_mrow[grp], i * 32 + 32)
                        wait(pe, s_exp, i * GROUPS * NEXP + n - 1)
                        col = 0
                        for j, kb in EXP_UNITS[u]:
                            pair, row = (grp * GH + j) // 2, 64 * (j % 2)
                            rows = stack[row:row + 64, pair]
                            width = T - kb * P
                            last = mm(e_bank[n % 2][:, col:col + width],
                                      rows[:, 1, kb * P:(kb + 1) * P], rows[:, 0, kb * P:],
                                      start=True, stop=True)
                            col += width
                        last.then_inc(s_efull, 1)
                    elif kind == "pv":
                        grp = w[1]
                        wait(pe, s_mask, i * GROUPS * NEXP + (grp + 1) * NEXP)
                        wait(pe, s_og, i * GROUPS + grp)
                        for kb in range(TB):
                            for j in range(GH):
                                c = PT_COL[(j, kb)]
                                last = mm(pv_bank[32 * j:32 * j + 32, kb * P:],
                                          v_sb[:, kb, grp * GH + j, :],
                                          pt[:, grp % 2, c:c + T - kb * P], start=(kb == 0),
                                          stop=(kb == TB - 1))
                        last.then_inc(s_pv, 1)
                    elif kind == "oT":
                        grp = w[1]
                        wait(pe, s_og, i * GROUPS + grp + 1)
                        four_transposes(b, lambda t: o_grp[:, grp % 2, t * P:(t + 1) * P],
                                        ident[:]).then_inc(s_vfull, 1)
                    elif kind == "OT":
                        wait(pe, s_vfree, unit)
                        four_transposes(b, lambda t: o_tok[:, t, :], ident[:]).then_inc(s_vfull, 1)
                    elif kind == "proj":
                        wait(pe, s_vfree, unit)
                        for t in range(TB):
                            last = mm(b[:, t * P:(t + 1) * P], oT[:, t * P:(t + 1) * P], wp[:],
                                      start=True, stop=True)
                        last.then_inc(s_vfull, 1)
                    elif kind == "x2T":
                        wait(pe, s_x2n, i * TB + TB)
                        four_transposes(b, lambda t: x2n[:, t, :], ident[:]).then_inc(s_vfull, 1)
                    elif kind == "z":
                        s = w[1]
                        if s == 0:
                            pe.wait_ge(s_wlo, 2)
                        wait(pe, s_hall, f * SLOTS + max(s - 1, 0))
                        if s == 1:
                            wait(pe, s_gtanh, f + 1)
                        split_matmul(z_bank[s % 2][:], w1_hi[:, s * P:(s + 1) * P],
                                     w1_lo[:, s * P:(s + 1) * P], x2T_hi[:],
                                     x2T_lo[:]).then_inc(s_z, 1)
                    elif kind == "yhi":
                        s = w[1]
                        wait(pe, s_hhi, f * SLOTS + s + 1)
                        if s % HC == 0:
                            wait(pe, s_yfree, f * NY + s // HC)
                        mm(y_bank[:], w2_lo[:, s * C:(s + 1) * C], h_hi[:, s % 2, :],
                           start=(s % HC == 0), stop=False)
                        mm(y_bank[:], w2_hi[:, s * C:(s + 1) * C], h_hi[:, s % 2, :],
                           start=False, stop=False).then_inc(s_yhi, 1)
                    elif kind == "ylo":
                        s = w[1]
                        split_done(pe, f, s)
                        mm(y_bank[:], w2_hi[:, s * C:(s + 1) * C], h_lo[:, s % 2, :],
                           start=False, stop=(s % HC == HC - 1)).then_inc(s_ylo, 1)
                    elif kind == "yT":
                        wait(pe, s_acc, (f + 1) * (EXPERTS - 1))
                        four_transposes(y_bank, lambda t: acc[:, t * P:(t + 1) * P],
                                        ident[:]).then_inc(s_yT, 1)

            steps_over_sequences(pe, step)




_INS = ["L0_attn_x", "L0_attn_w_qkv", "L0_attn_b_qkv", "L0_attn_w_proj", "L0_attn_b_proj",
        "L0_ffn_Wg", "L0_ffn_bg", "L0_ffn_W1", "L0_ffn_b1", "L0_ffn_W2", "L0_ffn_b2"]


def kernel(**inputs):
    import concourse.bacc as bacc
    from concourse.bass_utils import run_bass_kernel_spmd

    nc = bacc.Bacc("TRN2", target_bir_lowering=False, num_devices=1)
    arrays, args = {}, []
    for name in _INS:
        a = np.ascontiguousarray(inputs[name])
        arrays[f"in_{name}"] = a
        args.append(nc.dram_tensor(f"in_{name}", a.shape, mybir.dt.from_np(a.dtype),
                                   kind="ExternalInput").ap())
    out = nc.dram_tensor("out_x", (BATCH, T, C), F32, kind="ExternalOutput").ap()
    block_program(nc, *args, out)
    result = run_bass_kernel_spmd(nc, [arrays], core_ids=[0])
    return result.results[0]["out_x"]
```
